# Optimizing a Trainium2 kernel written in Bass

```python
import numpy as np
import jax
import jax.numpy as jnp

def _softmax(x, axis=-1):
    return jax.nn.softmax(x, axis=axis)

def _gelu(x):
    return jax.nn.gelu(x, approximate=True)

def _silu(x):
    return jax.nn.silu(x)

def _sigmoid(x):
    return jax.nn.sigmoid(x)

def _layernorm(x, axis=-1, eps=1e-05):
    m = jnp.mean(x, axis=axis, keepdims=True)
    v = jnp.var(x, axis=axis, keepdims=True)
    return (x - m) / jnp.sqrt(v + eps)

def _scatter_add(tgt, idx, src, axis=0):
    return tgt.at[idx].add(src)

def _segment_sum(src, seg, n):
    return jax.ops.segment_sum(src, seg, n)
kernel_name = 'mk_gnn_preln_d4_gnn_r64_d723df'

def setup_inputs(seed: int=0):
    np.random.seed(seed)
    _w = jnp.asarray

    def _rec_inputs():
        import jax
        import jax.numpy as jnp
        _gk = jax.random.key(seed)
        x = 0.4998 + 0.2887 * jax.random.normal(jax.random.fold_in(_gk, 1), (100000, 16), jnp.float32)
        src = jax.random.randint(jax.random.fold_in(_gk, 2), (50000,), 0, 100000, jnp.int32)
        dst = jnp.minimum((100000 * jax.random.uniform(jax.random.fold_in(_gk, 3), (50000,)) ** 2.0).astype(jnp.int32), 99999)
        _o = jnp.argsort(dst, stable=True)
        src = src[_o]
        dst = dst[_o]
        edge_attr_2 = 0.000411684 + 0.577418 * jax.random.normal(jax.random.fold_in(_gk, 11), (50000, 2), jnp.float32)
        edge_attr_8 = 0.000398945 + 1.00003 * jax.random.normal(jax.random.fold_in(_gk, 12), (50000, 8), jnp.float32)
        edge_weight = jax.random.uniform(jax.random.fold_in(_gk, 14), (50000,), jnp.float32, 0.0, 1)
        node_vec1 = -0.00472126 + 0.997171 * jax.random.normal(jax.random.fold_in(_gk, 15), (100000, 1), jnp.float32)
        return (x, src, dst, edge_attr_2, edge_attr_8, edge_weight, node_vec1)
    x, src, dst, edge_attr_2, edge_attr_8, edge_weight, node_vec1 = _rec_inputs()

    def _L0_gnn_setup():
        import jax, jax.numpy as jnp
        import numpy as np
        N_NODES = 100000
        key = jax.random.key(seed)
        k1, k2, k3, k4 = jax.random.split(key, 4)
        E = 50000
        D = 16
        x = jax.random.uniform(k1, (N_NODES, D), dtype=jnp.float32)
        edge_index = jax.random.randint(k2, (2, E), 0, N_NODES, dtype=jnp.int64)
        edge_probs = jax.random.uniform(k3, (E,), dtype=jnp.float32)
        weight = jnp.ones((D,), dtype=jnp.float32)
        self_loop_weight = jnp.asarray(0.1, dtype=jnp.float32)
        return {'x': x, 'edge_index': edge_index, 'edge_probs': edge_probs, 'weight': weight, 'self_loop_weight': self_loop_weight}
    _L0_gnn_all = _L0_gnn_setup()
    _L0_gnn_in = {k: v for k, v in _L0_gnn_all.items() if k in ('weight', 'self_loop_weight')}
    del _L0_gnn_all

    def _L1_gnn_setup():
        import jax, jax.numpy as jnp
        import numpy as np
        N_NODES = 100000
        N_EDGES = 25000
        F_IN = 16
        F_OUT = 16
        N_BASIS = 4

        def linear_basis(u, n):
            centers = jnp.linspace(-1.0, 1.0, n, dtype=u.dtype)
            dx = 2.0 / (n - 1)
            return jnp.maximum(0.0, 1.0 - jnp.abs(u[:, None] - centers[None, :]) / dx)
        key = jax.random.key(seed)
        k1, k2, k3, k4, k5 = jax.random.split(key, 5)
        x = jax.random.normal(k1, (N_NODES, F_IN), dtype=jnp.float32)
        edge_index = jax.random.randint(k2, (2, N_EDGES), 0, N_NODES, dtype=jnp.int64)
        edge_attr = jax.random.uniform(k3, (N_EDGES, 2), dtype=jnp.float32, minval=-1.0, maxval=1.0)
        weight = jax.random.uniform(k4, (N_BASIS, N_BASIS, F_IN, F_OUT), dtype=jnp.float32, minval=-0.05, maxval=0.05)
        return {'x': x, 'edge_index': edge_index, 'edge_attr': edge_attr, 'weight': weight}
    _L1_gnn_all = _L1_gnn_setup()
    _L1_gnn_in = {k: v for k, v in _L1_gnn_all.items() if k in ('weight',)}
    del _L1_gnn_all

    def _L2_gnn_setup():
        import jax, jax.numpy as jnp
        import numpy as np
        N = 100000
        E = 12500
        IN_C = 16
        OUT_C = 16
        HALF = OUT_C // 2
        T = 8
        EPS = 1e-05

        def _layernorm(x, g, b):
            mu = jnp.mean(x, axis=-1, keepdims=True)
            var = jnp.var(x, axis=-1, keepdims=True)
            return (x - mu) * jax.lax.rsqrt(var + EPS) * g + b

        def _edgeconv(x, edge_index, edge_attr, ln_g, ln_b, We, be, Wr, bias):
            h = jax.nn.relu(_layernorm(x, ln_g, ln_b))
            src, dst = (edge_index[0], edge_index[1])
            w = (edge_attr @ We + be).reshape(-1, IN_C, HALF)
            msg = jnp.einsum('ei,eio->eo', h[src], w)
            agg = jax.ops.segment_sum(msg, dst, num_segments=N)
            return agg + h @ Wr + bias
        key = jax.random.key(seed)
        ks = jax.random.split(key, 16)
        x = jax.random.normal(ks[0], (N, IN_C), dtype=jnp.float32)
        edge_index = jax.random.randint(ks[1], (2, E), 0, N, dtype=jnp.int64)
        edge_attr = jax.random.normal(ks[2], (E, T), dtype=jnp.float32)
        s_e = 1.0 / np.sqrt(T)
        s_r = 1.0 / np.sqrt(IN_C)
        params = {}
        for i, tag in enumerate(['n', 'r']):
            o = 3 + i * 6
            params['ln_g_' + tag] = jnp.ones((IN_C,), dtype=jnp.float32)
            params['ln_b_' + tag] = jnp.zeros((IN_C,), dtype=jnp.float32)
            params['We_' + tag] = jax.random.uniform(ks[o], (T, IN_C * HALF), minval=-s_e, maxval=s_e, dtype=jnp.float32)
            params['be_' + tag] = jax.random.uniform(ks[o + 1], (IN_C * HALF,), minval=-s_e, maxval=s_e, dtype=jnp.float32)
            params['Wr_' + tag] = jax.random.uniform(ks[o + 2], (IN_C, HALF), minval=-s_r, maxval=s_r, dtype=jnp.float32)
            params['b_' + tag] = jnp.zeros((HALF,), dtype=jnp.float32)
        return {'x': x, 'edge_index': edge_index, 'edge_attr': edge_attr, **params}
    _L2_gnn_all = _L2_gnn_setup()
    _L2_gnn_in = {k: v for k, v in _L2_gnn_all.items() if k in ('ln_g_n', 'ln_b_n', 'We_n', 'be_n', 'Wr_n', 'b_n', 'ln_g_r', 'ln_b_r', 'We_r', 'be_r', 'Wr_r', 'b_r')}
    del _L2_gnn_all

    def _L3_gnn_setup():
        import jax, jax.numpy as jnp
        import numpy as np
        N_NODES = 100000
        N_EDGES = 50000
        D_NODE = 16
        D_EDGE = 8
        D_HIDDEN = 16
        key = jax.random.key(seed)
        ks = jax.random.split(key, 8)
        node_features = jax.random.normal(ks[0], (N_NODES, D_NODE), dtype=jnp.float32)
        edge_attr_e3nn = jax.random.normal(ks[1], (N_EDGES, D_EDGE), dtype=jnp.float32)
        node_attr_scalar_raw = jax.random.normal(ks[2], (N_NODES, 1), dtype=jnp.float32)
        W_msg_tp = jax.random.normal(ks[3], (D_NODE, D_EDGE, D_HIDDEN), dtype=jnp.float32)
        W_msg_lin = jax.random.normal(ks[4], (D_HIDDEN, D_HIDDEN), dtype=jnp.float32)
        W_upd_tp = jax.random.normal(ks[5], (D_NODE, D_HIDDEN, D_HIDDEN), dtype=jnp.float32)
        W_upd_lin = jax.random.normal(ks[6], (D_HIDDEN, D_NODE), dtype=jnp.float32)
        edge_index = jax.random.randint(ks[7], (2, N_EDGES), 0, N_NODES, dtype=jnp.int64)
        return {'node_features': node_features, 'edge_attr_e3nn': edge_attr_e3nn, 'node_attr_scalar_raw': node_attr_scalar_raw, 'W_msg_tp': W_msg_tp, 'W_msg_lin': W_msg_lin, 'W_upd_tp': W_upd_tp, 'W_upd_lin': W_upd_lin, 'edge_index': edge_index}
    _L3_gnn_all = _L3_gnn_setup()
    _L3_gnn_in = {k: v for k, v in _L3_gnn_all.items() if k in ('W_msg_tp', 'W_msg_lin', 'W_upd_tp', 'W_upd_lin')}
    del _L3_gnn_all
    return {'x': x, 'src': src, 'dst': dst, 'edge_attr_2': edge_attr_2, 'edge_attr_8': edge_attr_8, 'edge_weight': edge_weight, 'node_vec1': node_vec1, 'L0_gnn_weight': _L0_gnn_in['weight'], 'L0_gnn_self_loop_weight': _L0_gnn_in['self_loop_weight'], 'L1_gnn_weight': _L1_gnn_in['weight'], 'L2_gnn_ln_g_n': _L2_gnn_in['ln_g_n'], 'L2_gnn_ln_b_n': _L2_gnn_in['ln_b_n'], 'L2_gnn_We_n': _L2_gnn_in['We_n'], 'L2_gnn_be_n': _L2_gnn_in['be_n'], 'L2_gnn_Wr_n': _L2_gnn_in['Wr_n'], 'L2_gnn_b_n': _L2_gnn_in['b_n'], 'L2_gnn_ln_g_r': _L2_gnn_in['ln_g_r'], 'L2_gnn_ln_b_r': _L2_gnn_in['ln_b_r'], 'L2_gnn_We_r': _L2_gnn_in['We_r'], 'L2_gnn_be_r': _L2_gnn_in['be_r'], 'L2_gnn_Wr_r': _L2_gnn_in['Wr_r'], 'L2_gnn_b_r': _L2_gnn_in['b_r'], 'L3_gnn_W_msg_tp': _L3_gnn_in['W_msg_tp'], 'L3_gnn_W_msg_lin': _L3_gnn_in['W_msg_lin'], 'L3_gnn_W_upd_tp': _L3_gnn_in['W_upd_tp'], 'L3_gnn_W_upd_lin': _L3_gnn_in['W_upd_lin']}

def reference(x, src, dst, edge_attr_2, edge_attr_8, edge_weight, node_vec1, L0_gnn_weight, L0_gnn_self_loop_weight, L1_gnn_weight, L2_gnn_ln_g_n, L2_gnn_ln_b_n, L2_gnn_We_n, L2_gnn_be_n, L2_gnn_Wr_n, L2_gnn_b_n, L2_gnn_ln_g_r, L2_gnn_ln_b_r, L2_gnn_We_r, L2_gnn_be_r, L2_gnn_Wr_r, L2_gnn_b_r, L3_gnn_W_msg_tp, L3_gnn_W_msg_lin, L3_gnn_W_upd_tp, L3_gnn_W_upd_lin):
    import jax
    import jax.numpy as jnp

    def _L0_gnn_ref(x, edge_index, edge_probs, weight, self_loop_weight):
        import jax, jax.numpy as jnp
        import numpy as np
        N_NODES = 100000
        src = edge_index[0]
        dst = edge_index[1]
        messages = x[src] * edge_probs[:, None] * weight
        out = jax.ops.segment_sum(messages, dst, num_segments=N_NODES)
        out = out + x * self_loop_weight
        return jnp.clip(x + out, 0.0, 1.0)

    def _L1_gnn_ref(x, edge_index, edge_attr, weight):
        import jax, jax.numpy as jnp
        import numpy as np
        N_NODES = 100000
        N_EDGES = 25000
        F_IN = 16
        F_OUT = 16
        N_BASIS = 4

        def linear_basis(u, n):
            centers = jnp.linspace(-1.0, 1.0, n, dtype=u.dtype)
            dx = 2.0 / (n - 1)
            return jnp.maximum(0.0, 1.0 - jnp.abs(u[:, None] - centers[None, :]) / dx)
        "BasisConvLayer forward, mode='conv', linear basis, no bias/activations.\n\n            For each edge e=(i<-j): msg_e = sum_{u,v} b_u(dx) b_v(dy) * (x_j @ W[u,v]);\n            out[i] = sum over incoming edges of msg_e.\n            "
        row, col = (edge_index[0], edge_index[1])
        x_j = x[col]
        bx = linear_basis(edge_attr[:, 0], N_BASIS)
        by = linear_basis(edge_attr[:, 1], N_BASIS)
        t = (bx[:, :, None] * by[:, None, :]).reshape(-1, N_BASIS * N_BASIS)
        w_flat = weight.reshape(N_BASIS * N_BASIS, F_IN, F_OUT)
        msg = jnp.zeros((x_j.shape[0], F_OUT), dtype=x.dtype)
        for k in range(N_BASIS * N_BASIS):
            msg = msg + t[:, k, None] * (x_j @ w_flat[k])
        out = jax.ops.segment_sum(msg, row, num_segments=N_NODES)
        return out

    def _L2_gnn_ref(x, edge_index, edge_attr, ln_g_n, ln_b_n, We_n, be_n, Wr_n, b_n, ln_g_r, ln_b_r, We_r, be_r, Wr_r, b_r):
        import jax, jax.numpy as jnp
        import numpy as np
        N = 100000
        E = 12500
        IN_C = 16
        OUT_C = 16
        HALF = OUT_C // 2
        T = 8
        EPS = 1e-05

        def _layernorm(x, g, b):
            mu = jnp.mean(x, axis=-1, keepdims=True)
            var = jnp.var(x, axis=-1, keepdims=True)
            return (x - mu) * jax.lax.rsqrt(var + EPS) * g + b

        def _edgeconv(x, edge_index, edge_attr, ln_g, ln_b, We, be, Wr, bias):
            h = jax.nn.relu(_layernorm(x, ln_g, ln_b))
            src, dst = (edge_index[0], edge_index[1])
            w = (edge_attr @ We + be).reshape(-1, IN_C, HALF)
            msg = jnp.einsum('ei,eio->eo', h[src], w)
            agg = jax.ops.segment_sum(msg, dst, num_segments=N)
            return agg + h @ Wr + bias
        edge_r = edge_index[:, ::-1]
        out_n = _edgeconv(x, edge_index, edge_attr, ln_g_n, ln_b_n, We_n, be_n, Wr_n, b_n)
        out_r = _edgeconv(x, edge_r, edge_attr, ln_g_r, ln_b_r, We_r, be_r, Wr_r, b_r)
        return jnp.concatenate([out_n, out_r], axis=-1)

    def _L3_gnn_ref(node_features, edge_attr_e3nn, node_attr_scalar_raw, W_msg_tp, W_msg_lin, W_upd_tp, W_upd_lin, edge_index):
        import jax, jax.numpy as jnp
        import numpy as np
        N_NODES = 100000
        N_EDGES = 50000
        D_NODE = 16
        D_EDGE = 8
        D_HIDDEN = 16
        n_nodes = node_features.shape[0]
        row = edge_index[0]
        col = edge_index[1]
        norm_msg_tp = 1.0 / np.float32(np.sqrt(D_NODE * D_EDGE))
        norm_upd_tp = 1.0 / np.float32(np.sqrt(D_NODE * D_HIDDEN))
        norm_lin = 1.0 / np.float32(np.sqrt(D_HIDDEN))
        x_j = node_features[col]
        m = jnp.einsum('ei,ej,ijh->eh', x_j, edge_attr_e3nn, W_msg_tp) * norm_msg_tp
        m = jax.nn.silu(m)
        m = m @ W_msg_lin * norm_lin
        agg = jax.ops.segment_sum(m, row, num_segments=n_nodes)
        u = jnp.einsum('ni,nh,ihk->nk', node_features, agg, W_upd_tp) * norm_upd_tp
        u = jax.nn.silu(u)
        u = u @ W_upd_lin * norm_lin
        return node_features + u
    edge_index = jnp.stack([src, dst])
    h = jnp.maximum(_layernorm(x, axis=-1), 0.0)
    x = x + _L0_gnn_ref(h, edge_index, edge_weight, L0_gnn_weight, L0_gnn_self_loop_weight)
    h = jnp.maximum(_layernorm(x, axis=-1), 0.0)
    x = x + _L1_gnn_ref(h, edge_index, edge_attr_2, L1_gnn_weight)
    h = jnp.maximum(_layernorm(x, axis=-1), 0.0)
    x = x + _L2_gnn_ref(h, edge_index, edge_attr_8, L2_gnn_ln_g_n, L2_gnn_ln_b_n, L2_gnn_We_n, L2_gnn_be_n, L2_gnn_Wr_n, L2_gnn_b_n, L2_gnn_ln_g_r, L2_gnn_ln_b_r, L2_gnn_We_r, L2_gnn_be_r, L2_gnn_Wr_r, L2_gnn_b_r)
    h = jnp.maximum(_layernorm(x, axis=-1), 0.0)
    x = x + _L3_gnn_ref(h, edge_attr_8, node_vec1, L3_gnn_W_msg_tp, L3_gnn_W_msg_lin, L3_gnn_W_upd_tp, L3_gnn_W_upd_lin, edge_index)
    return x

_drawn_inputs = setup_inputs


def setup_inputs(seed=0):
    import zlib

    import numpy as np

    out = dict(_drawn_inputs(seed))
    spreads = {'L0_gnn_weight': (1.0, 0.6),
     'L2_gnn_ln_g_n': (1.0, 0.2),
     'L2_gnn_ln_b_n': (0.0, 0.1),
     'L2_gnn_b_n': (0.0, 0.1),
     'L2_gnn_ln_g_r': (1.0, 0.2),
     'L2_gnn_ln_b_r': (0.0, 0.1),
     'L2_gnn_b_r': (0.0, 0.1)}
    factors = {}
    for name, (base, spread) in spreads.items():
        noise = np.random.default_rng([zlib.crc32(name.encode()), seed]).standard_normal(out[name].shape)
        drawn = base * np.exp(spread * noise) if base else spread * noise
        out[name] = jnp.asarray(drawn.astype(out[name].dtype))
    for name, factor in factors.items():
        out[name] = (out[name] * factor).astype(out[name].dtype)
    return out
```

```python
import concourse.bass as bass
from concourse import mybir
from contextlib import ExitStack


P = 128
N, E, D = 100000, 50000, 16
COLS = 784
NPAD = P * COLS
ROWS = NPAD + P
CH = 112
NCH = COLS // CH
CW = CH * D
RB = 7
BLK = CW // P
FULL = N // COLS
LAST = N - FULL * COLS
WIDE = FULL // 16 * 16
ZW = 448
U = 14
TILES = 392
GROUPS = TILES // U
PAIRS = GROUPS // 2
ET = E // P
REST = E - ET * P
AHEAD = 2
ICOLS = TILES + AHEAD * U
T2 = 8
A9 = T2 + 1
HALF = 8
EPS = 1e-5


class Steps:

    def __init__(self, eng, sem):
        self.eng, self.sem, self.base, self.turn, self.per, self.k = eng, sem, 0, 0, 0, 0

    def begin(self, turn, per):
        self.turn, self.per, self.k = turn, per, 0

    def end(self, turns):
        assert self.k == self.per, (self.k, self.per)
        self.base += self.per * turns
        self.begin(0, 0)

    def did(self, instruction):
        self.k += 1
        instruction.then_inc(self.sem, 1)

    def settle(self, but=0):
        self.eng.wait_ge(self.sem, self.turn * self.per + (self.base + self.k - but))


def build_gnn(nc, x_in, src_in, dst_in, attr2_in, attr8_in, attr8_rev_in, ew_in, vec1_in, w0_in, slw_in, w1_in,
              g_n_in, b_n_in, We_n_in, be_n_in, Wr_n_in, bias_n_in,
              g_r_in, b_r_in, We_r_in, be_r_in, Wr_r_in, bias_r_in,
              Wmsg_in, Wmlin_in, Wupd_in, Wulin_in, out):
    f32, i32 = mybir.dt.float32, mybir.dt.int32
    ALU, ACT, AX = mybir.AluOpType, mybir.ActivationFunctionType, mybir.AxisListType
    NORM_MSG = float((D * T2) ** -0.5)
    NORM_UPD = float((D * D) ** -0.5)
    NORM_LIN = float(D ** -0.5)

    ctx = ExitStack()
    with ctx:
        def sb(name, shape, dt=f32):
            return ctx.enter_context(nc.sbuf_tensor(name, shape, dt))

        def sem(name):
            return ctx.enter_context(nc.semaphore(name))

        table = nc.dram_tensor("table", (ROWS, D), f32)
        accum = [[nc.dram_tensor(f"accum{l}_{s}", (ROWS, D), f32) for s in range(2)]
                 for l in range(4)]

        x = sb("x", [P, COLS * D])
        h = sb("h", [P, COLS * D])
        src = sb("src", [P, ICOLS], i32)
        dst = sb("dst", [P, ICOLS], i32)
        to_src = sb("to_src", [P, TILES], i32)
        to_dst = sb("to_dst", [P, TILES], i32)
        ew = sb("ew", [P, TILES])
        attr2 = sb("attr2", [P, TILES * 2])
        attr8 = sb("attr8", [P, TILES * T2])
        rev8 = [sb(f"rev8_{p}", [P, U * T2]) for p in range(2)]
        gidx = [sb(f"gidx{p}", [P, U], i32) for p in range(2)]
        sidx = [sb(f"sidx{p}", [P, U], i32) for p in range(2)]
        rows = [sb(f"rows{p}", [P, 2 * P]) for p in range(2)]
        msgs = [sb(f"msgs{p}", [P, U * D]) for p in range(2)]
        key = sb("key", [P, U])
        same = sb("same", [P, CW])
        tB = sb("tB", [P, CW])
        prod = sb("prod", [P, 2 * CW])
        raw = sb("raw", [P, U * D])
        small = sb("small", [P, 4 * CH])
        basis = sb("basis", [P, U * D])
        feat = sb("feat", [P, 4 * P])
        featT = sb("featT", [P, 4 * P])
        ident = sb("ident", [P, P])
        lower = sb("lower", [P, P])
        rowmask = sb("rowmask", [P, 8])
        pad_row = sb("pad_row", [P, 1])
        eps = sb("eps", [P, 1])
        w0 = sb("w0", [P, D])
        slw1 = sb("slw1", [P, 1])
        gains = [sb(f"gain{s}", [P, D]) for s in range(2)]
        shifts = [sb(f"shift{s}", [P, D]) for s in range(2)]
        bias16 = sb("bias16", [P, D])
        W1 = sb("W1", [P, 4 * 512])
        W2 = [sb(f"W2_{s}", [P, 2 * 288]) for s in range(2)]
        W3 = sb("W3", [P, 2 * 512])
        Wroot = [sb(f"Wroot{s}", [P, P]) for s in range(2)]
        W4 = W1
        Wfin = sb("Wfin", [P, P])
        mlinT = sb("mlinT", [D, P])
        upd = sb("upd", [D, D * D])

        zeros = sb("zeros", [P, ZW])
        rt = sb("rt", [P, 2 * CW])

        psK = ctx.enter_context(nc.psum_tensor("psK", [P, 2048], f32))
        psT = ctx.enter_context(nc.psum_tensor("psT", [P, 512], f32))
        psP = [ctx.enter_context(nc.psum_tensor(f"psP{i}", [P, 512], f32)) for i in range(2)]
        psM = ctx.enter_context(nc.psum_tensor("psM", [P, 512], f32))

        loaded = sem("loaded")
        cleared = sem("cleared")
        masks = sem("masks")
        w4_ready = sem("w4_ready")
        w4_psum = sem("w4_psum")
        zeroed = [sem(f"zeroed{l}") for l in range(4)]
        stored = sem("stored")
        names = ("staged",
                 "go",
                 "key",
                 "keyT",
                 "same",
                 "feat",
                 "bandT",
                 "bandS",
                 "prod",
                 "used",
                 "preact",
                 "expo",
                 "raw",
                 "sum",
                 "msg")
        ed = [{n: sem(f"e{l}_{n}") for n in names} for l in range(4)]
        rev_in = [sem(f"rev_in{p}") for p in range(2)]
        rev_rest = sem("rev_rest")
        gath = [[sem(f"e{l}_gath{p}") for p in range(2)] for l in range(4)]
        scat = [[sem(f"e{l}_scat{s}") for s in range(2)] for l in range(4)]
        nnames = ("load",
                  "taken",
                  "center",
                  "square",
                  "varsum",
                  "sdev",
                  "norm",
                  "store")
        nd = [{n: sem(f"n{l}_{n}") for n in nnames} for l in range(4)]
        unames = ("load", "taken",
                  "sumT", "sumS",
                  "prod", "used",
                  "preact", "expo", "silu",
                  "siluT", "siluS",
                  "update",
                  "done")
        up = {n: sem(f"u_{n}") for n in unames}
        rnames = ("feat", "bandT", "bandS", "root")
        rt_s = {n: sem(f"r_{n}") for n in rnames}
        dve_go = sem("dve_go")
        dve_step = sem("dve_step")

        def v3(ap, f=D):
            return ap.rearrange("p (u f) -> p u f", f=f)

        def node_rows(t, w=D):
            return t.ap()[0:NPAD, :].rearrange("(p c) f -> p (c f)", p=P)

        tA, tC, tD = same, prod[:, 0:CW], prod[:, CW:2 * CW]
        load_incs = [0]
        MASKS = 9
        STEPS = [14, 26, 16, 6]
        LOADS = 16 * 102
        CLEARED = 22

        block = ctx.enter_context(nc.Block())

        GATHER = [src, dst, src, dst]
        KEY = [dst, src, dst, src]
        TO = [to_dst, to_src, to_dst, to_src]
        GATH = 16 * U
        SCAT = 16 * U // 2
        FREE = 16

        @block.sync
        def _(sp):
            def load(o, i):
                load_incs[0] += 16
                sp.dma_start(o, i).then_inc(loaded, 16)

            sp.wait_ge(cleared, CLEARED)
            sp.wait_ge(masks, MASKS)
            for a, b in ((0, WIDE), (WIDE, FULL)):
                load(x[a:b, :], x_in[a * COLS:b * COLS, :].rearrange("(p c) f -> p (c f)", c=COLS))
            load(x[FULL:FULL + 1, 0:LAST * D],
                 x_in[FULL * COLS:N, :].rearrange("(p c) f -> p (c f)", p=1))
            with nc.allow_non_contiguous_dma(reason="the last column of edges and small weights"):
                for t, a, w in ((src, src_in, 1), (dst, dst_in, 1), (ew, ew_in, 1)):
                    load(t[:, 0:ET], a[0:ET * P].rearrange("(p c) -> p c", p=P))
                    load(t[0:REST, ET:ET + 1], a[ET * P:E].rearrange("(p c) -> p c", c=1))
                a2, a8 = v3(attr2[:, :], 2), v3(attr8[:, :], T2)
                load(a2[:, 0:ET, :], attr2_in[0:ET * P, :].rearrange("(p c) f -> p c f", p=P))
                load(a2[0:REST, ET, :], attr2_in[ET * P:E, :])
                load(a8[:, 0:ET, :], attr8_in[0:ET * P, :].rearrange("(p c) f -> p c f", p=P))
                load(a8[0:REST, ET, :], attr8_in[ET * P:E, :])
                load(w0[:, :], w0_in[None, :].to_broadcast([P, D]))
                load(slw1[:, :], slw_in[None, :].to_broadcast([P, 1]))
                for s, (g, b) in enumerate(((g_n_in, b_n_in), (g_r_in, b_r_in))):
                    load(gains[s][:, :], g[None, :].to_broadcast([P, D]))
                    load(shifts[s][:, :], b[None, :].to_broadcast([P, D]))
                load(bias16[:, 0:HALF], bias_n_in[None, :].to_broadcast([P, HALF]))
                load(bias16[:, HALF:D], bias_r_in[None, :].to_broadcast([P, HALF]))
                w1v = w1_in.rearrange("a b i o -> i (a b) o")
                w3v = Wmsg_in.rearrange("i j h -> i (j h)")
                for v in range(8):
                    band = slice(D * v, D * v + D)
                    c1 = (v // 2) * 512 + (v % 2) * 256
                    load(v3(W1[:, :])[band, c1 // D:c1 // D + D, :], w1v)
                    c3 = v * P
                    load(W3[band, c3:c3 + P], w3v)
                    for s, (We, be, Wr) in enumerate(((We_n_in, be_n_in, Wr_n_in),
                                                      (We_r_in, be_r_in, Wr_r_in))):
                        c2 = v * A9
                        w2 = v3(W2[s][:, :], HALF)
                        load(w2[band, c2:c2 + T2, :], We.rearrange("t (i o) -> i t o", o=HALF))
                        load(w2[band, c2 + T2, :], be.rearrange("(i o) -> i o", o=HALF))
                        load(Wroot[s][band, v * D + s * HALF:v * D + (s + 1) * HALF], Wr)
                    load(Wfin[band, v * D:v * D + D], Wulin_in)
                    load(mlinT[:, band], Wmlin_in.rearrange("q h -> h q"))
                load(v3(upd[:, :]), Wupd_in.rearrange("i h k -> h i k"))

            assert load_incs[0] == LOADS, load_incs

            def zero(l):
                for s in range(2):
                    times = COLS * D // ZW
                    sp.dma_start(accum[l][s].ap()[0:NPAD, :].rearrange("(p k c) f -> p k (c f)", p=P, k=times),
                                 zeros[:, None, :].to_broadcast([P, times, ZW])).then_inc(zeroed[l], 16)

            sp.dma_start(table.ap()[NPAD:ROWS, :], zeros[:, 0:D]).then_inc(zeroed[0], 16)
            zero(0)
            for l in range(4):
                if l == 2:
                    rev = attr8_rev_in[0:ET * P, :].rearrange("(p c) f -> p (c f)", p=P)

                    def reverse(par, col, cols=U):
                        sp.dma_start(rev8[par][:, 0:cols * T2], rev[:, bass.ds(col * T2, cols * T2)])\
                            .then_inc(rev_in[par], 16)

                    reverse(0, 0)
                    reverse(1, U)
                if l < 3:
                    sp.wait_ge(ed[l]["msg"], 1)
                    zero(l + 1)
                if l == 2:
                    with sp.Fori(1, PAIRS - 1) as c:
                        for par in range(2):
                            sp.wait_ge(ed[l]["msg"], 2 * c + (par - 1))
                            reverse(par, (2 * c + par) * U)
                    sp.wait_ge(ed[l]["msg"], GROUPS - 3)
                    reverse(0, (GROUPS - 2) * U)
                    sp.wait_ge(ed[l]["msg"], GROUPS - 2)
                    left = ET - (GROUPS - 1) * U
                    sp.dma_start(rev8[1][0:REST, left * T2:(left + 1) * T2], attr8_rev_in[ET * P:E, :])\
                        .then_inc(rev_rest, 16)
                    sp.wait_ge(rev_rest, 16)
                    reverse(1, (GROUPS - 1) * U, left)
                for s in range(2):
                    sp.wait_ge(scat[l][s], FREE + SCAT * GROUPS)
                n = nd[l + 1] if l < 3 else up

                def fetch(c):
                    for s, t in enumerate((tA, tB)):
                        sp.dma_start(t[:, :], node_rows(accum[l][s])[:, bass.ds(c * CW, CW)])\
                            .then_inc(n["load"], 16)

                fetch(0)
                with sp.Fori(1, NCH) as c:
                    sp.wait_ge(n["taken"], c)
                    fetch(c)

        @block.gpsimd
        def _(pool):
            pool.memset(ident[:, :], 0.0).then_inc(masks, 1)
            pool.memset(lower[:, :], 1.0).then_inc(masks, 1)
            pool.memset(rowmask[:, :], 1.0).then_inc(masks, 1)
            for t in (src, dst):
                pool.iota(t[:, ET:ICOLS], pattern=[[0, ICOLS - ET]], base=NPAD, channel_multiplier=1)\
                    .then_inc(masks, 1)
            pool.wait_ge(masks, 3)
            pool.affine_select(out=ident[:, :], in_=ident[:, :], compare_op=ALU.not_equal, fill=1.0, base=0,
                               pattern=[[-1, P]], channel_multiplier=1).then_inc(masks, 1)
            pool.affine_select(out=lower[:, :], in_=lower[:, :], compare_op=ALU.is_gt, fill=0.0, base=0,
                               pattern=[[-1, P]], channel_multiplier=1).then_inc(masks, 1)
            pool.affine_select(out=rowmask[:, :], in_=rowmask[:, :], compare_op=ALU.is_ge, fill=0.0, base=0,
                               pattern=[[-D, 8]], channel_multiplier=1).then_inc(masks, 1)
            pool.wait_ge(masks, MASKS - 1)
            pool.affine_select(out=rowmask[:, :], in_=rowmask[:, :], compare_op=ALU.is_ge, fill=0.0, base=D - 1,
                               pattern=[[D, 8]], channel_multiplier=-1).then_inc(masks, 1)

            for l in range(4):
                e = ed[l]

                def gather(par):
                    for u in range(U):
                        pool.indirect_dma_start(
                            out=rows[par][:, u * D:(u + 1) * D], out_offset=None, in_=table.ap(),
                            in_offset=bass.IndirectOffsetOnAxis(ap=gidx[par][:, u:u + 1], axis=0))\
                            .then_inc(gath[l][par], 16)

                def scatter(par, turn):
                    for u in range(U):
                        pool.wait_ge(scat[l][u % 2], turn * (2 * SCAT) + (FREE + par * SCAT + 16 * (u // 2)))
                        pool.sem_inc(e["go"], 1)
                        pool.indirect_dma_start(
                            out=accum[l][u % 2].ap(),
                            out_offset=bass.IndirectOffsetOnAxis(ap=sidx[par][:, u:u + 1], axis=0),
                            in_=msgs[par][:, u * D:(u + 1) * D], in_offset=None, compute_op=ALU.add)\
                            .then_inc(scat[l][u % 2], 16)

                pool.wait_ge(cleared, CLEARED)
                for s in range(2):
                    pool.dma_start(accum[l][s].ap()[NPAD:ROWS, :], zeros[:, 0:D]).then_inc(scat[l][s], FREE)
                pool.wait_ge(nd[l]["store"], 16 * NCH)
                pool.wait_ge(e["staged"], 2)
                if l == 0:
                    pool.wait_ge(zeroed[0], 16 * 3)
                pool.sem_inc(e["go"], 1)
                gather(0)
                gather(1)
                if l:
                    pool.wait_ge(zeroed[l], 16 * 2)
                with pool.Fori(0, PAIRS - 1) as c:
                    for par in range(2):
                        pool.wait_ge(e["msg"], 2 * c + (par + 1))
                        pool.sem_inc(e["go"], 1)
                        scatter(par, c)
                        gather(par)
                for par in range(2):
                    pool.wait_ge(e["msg"], 2 * (PAIRS - 1) + par + 1)
                    scatter(par, PAIRS - 1)

        @block.tensor
        def _(pe):
            pe.wait_ge(masks, MASKS)
            pe.wait_ge(loaded, LOADS)
            for l in range(4):
                e = ed[l]
                with pe.Fori(0, PAIRS) as c:
                    for par in range(2):
                        pe.wait_ge(e["key"], 2 * c + (par + 1))
                        for u in range(U):
                            k = nc.tensor.transpose(psK[:, u * P:(u + 1) * P],
                                                    key[:, u:u + 1].to_broadcast([P, P]), ident[:, :])
                        k.then_inc(e["keyT"], 1)
                        if l:
                            if l == 2:
                                pe.wait_ge(e["feat"], 2 * c + (par + 1))
                                bands = [feat[:, b * P:(b + 1) * P] for b in range(4)]
                            else:
                                pe.wait_ge(gath[l][par], c * GATH + GATH)
                                bands = [rows[par][:, b * P:(b + 1) * P] for b in range(2)]
                            for b, band in enumerate(bands):
                                k = nc.tensor.transpose(psT[:, b * P:(b + 1) * P], band, ident[:, :])
                            k.then_inc(e["bandT"], 1)
                            pe.wait_ge(e["bandS"], 2 * c + (par + 1))
                            if l == 1:
                                parts = [(m // 4, W1[:, (m % 4) * 512:(m % 4 + 1) * 512]) for m in range(7)]
                            elif l == 3:
                                parts = [(m // 2, W3[:, (m % 2) * 512:(m % 2 + 1) * 512]) for m in range(4)]
                            else:
                                parts = [(2 * s + m // 2, W2[s][:, (m % 2) * 288:(m % 2 + 1) * 288])
                                         for s in range(2) for m in range(4)]
                            n = len(parts)
                            for m, (b, w) in enumerate(parts):
                                if m >= 2:
                                    pe.wait_ge(e["used"], c * (2 * n) + (par * n + m - 1))
                                nc.tensor.matmul(psP[m % 2][:, 0:w.shape[1]], featT[:, b * P:(b + 1) * P], w,
                                                 start=True, stop=True).then_inc(e["prod"], 1)
                        pe.wait_ge(e["same"], 2 * c + (par + 1))
                        pe.wait_ge(e["raw"], 2 * c + (par + 1))
                        for u in range(U):
                            k = nc.tensor.matmul(psM[:, u * D:(u + 1) * D], same[:, u * P:(u + 1) * P],
                                                 raw[:, u * D:(u + 1) * D], start=True, stop=True)
                        k.then_inc(e["sum"], 1)
                    if l == 2:
                        for s in range(2):
                            pe.wait_ge(rt_s["feat"], 2 * c + (s + 1))
                            if s:
                                pe.wait_ge(rt_s["bandS"], 2 * c + s)
                            for b in range(RB):
                                k = nc.tensor.transpose(psK[:, b * P:(b + 1) * P],
                                                        rt[:, (s * RB + b) * P:(s * RB + b + 1) * P], ident[:, :])
                            k.then_inc(rt_s["bandT"], 1)
                        pe.wait_ge(rt_s["bandS"], 2 * c + 2)
                        for b in range(RB):
                            for s in range(2):
                                k = nc.tensor.matmul(psK[:, b * P:(b + 1) * P],
                                                     rt[:, ((2 + s) * RB + b) * P:((2 + s) * RB + b + 1) * P],
                                                     Wroot[s][:, :], start=s == 0, stop=s == 1)
                        k.then_inc(rt_s["root"], 1)

                if l == 1:
                    pe.wait_ge(e["msg"], GROUPS)
                    nc.tensor.matmul(psM[:, 0:256], mlinT[:, :], upd[:, :], start=True, stop=True)\
                        .then_inc(w4_psum, 1)
                    pe.wait_ge(w4_ready, 1)

            with pe.Fori(0, NCH) as c:
                pe.wait_ge(up["taken"], c + 1)
                for b in range(BLK):
                    k = nc.tensor.transpose(psK[:, b * P:(b + 1) * P], tC[:, b * P:(b + 1) * P], ident[:, :])
                k.then_inc(up["sumT"], 1)
                pe.wait_ge(up["sumS"], c + 1)
                for m in range(4 * BLK):
                    b, j = m // 4, m % 4
                    if m >= 2:
                        pe.wait_ge(up["used"], c * (4 * BLK) + (m - 1))
                    nc.tensor.matmul(psP[m % 2][:, :], rt[:, b * P:(b + 1) * P], W4[:, j * 512:(j + 1) * 512],
                                     start=True, stop=True).then_inc(up["prod"], 1)
                pe.wait_ge(up["silu"], c + 1)
                for b in range(BLK):
                    k = nc.tensor.transpose(psK[:, b * P:(b + 1) * P], tC[:, b * P:(b + 1) * P], ident[:, :])
                k.then_inc(up["siluT"], 1)
                pe.wait_ge(up["siluS"], c + 1)
                for b in range(BLK):
                    k = nc.tensor.matmul(psK[:, b * P:(b + 1) * P], rt[:, CW + b * P:CW + (b + 1) * P], Wfin[:, :],
                                         start=True, stop=True)
                k.then_inc(up["update"], 1)

        @block.scalar
        def _(act):
            for d in range(4):
                n, e, times = nd[d], ed[d], 2 if d == 2 else 1
                with act.Fori(0, NCH) as c:
                    for k in range(times):
                        act.wait_ge(n["center"], c * times + (k + 1))
                        nc.scalar.activation(tD, tC, ACT.Square).then_inc(n["square"], 1)
                        act.wait_ge(n["varsum"], c * times + (k + 1))
                        nc.scalar.activation(small[:, CH:2 * CH], small[:, 0:CH], ACT.Sqrt, bias=eps[:, :],
                                             scale=1.0 / D).then_inc(n["sdev"], 1)
                    act.wait_ge(n["norm"], c * times + times)
                    act.dma_start(node_rows(table)[:, bass.ds(c * CW, CW)], h[:, bass.ds(c * CW, CW)])\
                        .then_inc(n["store"], 16)
                if d:
                    with act.Fori(0, PAIRS) as c:
                        for par in range(2):
                            w = 4 * P if d == 2 else 2 * P
                            act.wait_ge(e["bandT"], 2 * c + (par + 1))
                            nc.scalar.activation(featT[:, 0:w], psT[:, 0:w], ACT.Copy).then_inc(e["bandS"], 1)
                            if d == 3:
                                act.wait_ge(e["preact"], 2 * c + (par + 1))
                                nc.scalar.activation(basis[:, :], raw[:, :], ACT.Exp, scale=-NORM_MSG)\
                                    .then_inc(e["expo"], 1)
                        if d == 2:
                            for s in range(2):
                                act.wait_ge(rt_s["bandT"], 2 * c + (s + 1))
                                nc.scalar.activation(rt[:, (2 + s) * RB * P:(3 + s) * RB * P], psK[:, 0:RB * P],
                                                     ACT.Copy).then_inc(rt_s["bandS"], 1)
            with act.Fori(0, NCH) as c:
                act.wait_ge(up["sumT"], c + 1)
                nc.scalar.activation(rt[:, 0:CW], psK[:, 0:CW], ACT.Copy).then_inc(up["sumS"], 1)
                act.wait_ge(up["preact"], c + 1)
                nc.scalar.activation(tC, tD, ACT.Exp, scale=-NORM_UPD).then_inc(up["expo"], 1)
                act.wait_ge(up["siluT"], c + 1)
                nc.scalar.activation(rt[:, CW:2 * CW], psK[:, 0:CW], ACT.Copy).then_inc(up["siluS"], 1)
                act.wait_ge(up["done"], c + 1)
                for a, b in ((0, WIDE), (WIDE, FULL)):
                    act.dma_start(out[a * COLS:b * COLS, :].rearrange("(p c) f -> p (c f)", c=COLS)
                                  [:, bass.ds(c * CW, CW)], x[a:b, bass.ds(c * CW, CW)]).then_inc(stored, 16)
            act.dma_start(out[FULL * COLS:N, :].rearrange("(p c) f -> p (c f)", p=1),
                          x[FULL:FULL + 1, 0:LAST * D]).then_inc(stored, 16)
            act.wait_ge(stored, 16 * (2 * NCH + 1))

        @block.vector
        def _(dve):
            V = nc.vector
            own = Steps(dve, dve_step)

            def clear(t, value=0.0):
                V.memset(t, value).then_inc(cleared, 1)

            clear(zeros[:, :])
            clear(x[96:P, LAST * D:])
            clear(ew[:, ET:])
            clear(attr2[:, 2 * ET:])
            clear(attr8[:, T2 * ET:])
            clear(feat[:, :])
            for par in range(2):
                clear(rows[par][:, :])
                clear(rev8[par][:, :])
            for t in (W1, W2[0], W2[1], W3, Wroot[0], Wroot[1], Wfin):
                clear(t[:, :])
            clear(eps[:, :], EPS)
            clear(key[:, :])
            clear(raw[:, :])
            clear(small[:, :])
            clear(msgs[0][:, :])

            dve.wait_ge(loaded, LOADS)
            own.begin(0, 2)
            own.did(V.tensor_copy(pad_row[:, :], dst[:, ICOLS - 1:ICOLS]))
            own.did(V.tensor_scalar_add(slw1[:, :], slw1[:, :], 1.0))
            own.settle()
            own.end(1)

            mu, inv = small[:, 2 * CH:3 * CH], small[:, 3 * CH:4 * CH]

            def spread(ap, f=D):
                return ap[:, :, None].to_broadcast([P, ap.shape[1], f])

            def normalize(n, xs, hs, turn, relu):
                dve.sem_inc(dve_go, 1)
                own.did(V.tensor_reduce(mu, v3(xs), AX.X, ALU.add))
                own.settle()
                V.scalar_tensor_tensor(v3(tC), spread(mu), -1.0 / D, v3(xs), ALU.mult, ALU.add)\
                    .then_inc(n["center"], 1)
                dve.wait_ge(n["square"], turn + 1)
                V.tensor_reduce(small[:, 0:CH], v3(tD), AX.X, ALU.add).then_inc(n["varsum"], 1)
                dve.wait_ge(n["sdev"], turn + 1)
                own.did(V.reciprocal(inv, small[:, CH:2 * CH]))
                own.settle()
                if relu:
                    V.scalar_tensor_tensor(v3(hs), v3(tC), 0.0, spread(inv), ALU.max, ALU.mult)\
                        .then_inc(n["norm"], 1)
                else:
                    V.tensor_tensor(v3(hs), v3(tC), spread(inv), ALU.mult).then_inc(n["norm"], 1)

            def node_phase(d):
                n = nd[d]
                with dve.Fori(0, NCH) as c:
                    own.begin(c, (2, 5, 5, 3)[d])
                    xs, hs = x[:, bass.ds(c * CW, CW)], h[:, bass.ds(c * CW, CW)]
                    if d:
                        dve.wait_ge(n["load"], 32 * c + 32)
                    if d == 1:
                        V.tensor_tensor(tC, tA[:, :], tB[:, :], ALU.add).then_inc(n["taken"], 1)
                        dve.wait_ge(n["taken"], c + 1)
                        own.did(V.scalar_tensor_tensor(tC, hs, slw1[:, :], tC, ALU.mult, ALU.add))
                        own.settle()
                        own.did(V.tensor_scalar(tC, tC, 0.0, 1.0, ALU.max, ALU.min))
                        own.settle()
                        own.did(V.tensor_tensor(xs, xs, tC, ALU.add))
                        own.settle()
                    elif d:
                        V.tensor_tensor(tC, tA[:, :], tB[:, :], ALU.add).then_inc(n["taken"], 1)
                        dve.wait_ge(n["taken"], c + 1)
                        own.did(V.tensor_tensor(xs, xs, tC, ALU.add))
                        own.settle()
                    if d == 2:
                        normalize(n, xs, hs, 2 * c, True)
                        dve.wait_ge(n["norm"], 2 * c + 1)
                        normalize(n, hs, hs, 2 * c + 1, False)
                        dve.wait_ge(n["norm"], 2 * c + 2)
                    else:
                        normalize(n, xs, hs, c, True)
                        dve.wait_ge(n["norm"], c + 1)
                own.end(NCH)

            def stage(l, par, col):
                return V.tensor_copy(gidx[par][:, :], GATHER[l][:, bass.ds(col, U)])

            def messages(l, c, par, col):
                e = ed[l]
                if l == 0:
                    own.did(V.tensor_tensor(v3(basis[:, :]), v3(rows[par][:, 0:U * D]),
                                            spread(ew[:, bass.ds(col, U)]), ALU.mult))
                    own.settle()
                    V.tensor_tensor(v3(raw[:, :]), v3(basis[:, :]), w0[:, None, :].to_broadcast([P, U, D]),
                                    ALU.mult).then_inc(e["raw"], 1)
                elif l == 1:
                    uv = attr2[:, bass.ds(col * 2, 2 * U)]
                    hats = small[:, 0:8 * U]
                    for k in range(4):
                        own.did(V.tensor_scalar(v3(hats, 4)[:, :, k], uv, -1.0 + 2.0 * k / 3.0, 1.5,
                                                ALU.subtract, ALU.mult))
                    own.settle()
                    own.did(V.scalar_tensor_tensor(hats, hats, -1.0, hats, ALU.mult, ALU.min))
                    own.settle()
                    own.did(V.tensor_scalar(hats, hats, 1.0, 0.0, ALU.add, ALU.max))
                    own.settle()
                    hv = hats.rearrange("p (u c n) -> p u c n", c=2, n=4)
                    own.did(V.tensor_tensor(basis[:, :].rearrange("p (u a b) -> p u a b", a=4, b=4),
                                            hv[:, :, 0, :, None].to_broadcast([P, U, 4, 4]),
                                            hv[:, :, 1, None, :].to_broadcast([P, U, 4, 4]), ALU.mult))
                    own.settle()
                    for m in range(7):
                        dve.wait_ge(e["prod"], 14 * c + (7 * par + m + 1))
                        V.tensor_tensor(v3(prod[:, m * 512:(m + 1) * 512]), v3(psP[m % 2][:, :]),
                                        spread(basis[:, 32 * m:32 * m + 32]), ALU.mult).then_inc(e["used"], 1)
                    dve.wait_ge(e["used"], 14 * c + (7 * par + 7))
                    V.tensor_reduce(v3(raw[:, :]), prod[:, :].rearrange("p (u k o) -> p u o k", k=D, o=D),
                                    AX.X, ALU.add).then_inc(e["raw"], 1)
                elif l == 2:
                    dve.wait_ge(rev_in[par], 16 * c + 16)
                    for m in range(8):
                        s, q = m // 4, m % 4
                        tiles = min(4, U - 4 * q)
                        dve.wait_ge(e["prod"], 16 * c + (8 * par + m + 1))
                        o = s * CW + q * 288
                        ps = psP[m % 2][:, 0:tiles * 72].rearrange("p (u t o) -> p u t o", t=A9, o=HALF)
                        pr = prod[:, o:o + tiles * 72].rearrange("p (u t o) -> p u t o", t=A9, o=HALF)
                        at = (rev8[par][:, 4 * q * T2:(4 * q + tiles) * T2] if s
                              else attr8[:, bass.ds(col * T2 + 4 * q * T2, T2 * tiles)])
                        V.tensor_tensor(pr[:, :, 0:T2, :], ps[:, :, 0:T2, :],
                                        v3(at, T2)[:, :, :, None].to_broadcast([P, tiles, T2, HALF]), ALU.mult)
                        V.tensor_copy(pr[:, :, T2, :], ps[:, :, T2, :]).then_inc(e["used"], 1)
                    dve.wait_ge(e["used"], 16 * c + (8 * par + 8))
                    for s in range(2):
                        k = V.tensor_reduce(v3(raw[:, :])[:, :, s * HALF:(s + 1) * HALF],
                                            prod[:, s * CW:s * CW + U * 72]
                                            .rearrange("p (u t o) -> p u o t", t=A9, o=HALF), AX.X, ALU.add)
                    k.then_inc(e["raw"], 1)
                else:
                    for m in range(4):
                        tiles = min(4, U - 4 * m)
                        dve.wait_ge(e["prod"], 8 * c + (4 * par + m + 1))
                        av = v3(attr8[:, bass.ds(col * T2 + 4 * m * T2, T2 * tiles)], T2)[:, :, :, None]
                        V.tensor_tensor(prod[:, m * 512:m * 512 + tiles * P]
                                        .rearrange("p (u j h) -> p u j h", j=T2, h=D),
                                        psP[m % 2][:, 0:tiles * P].rearrange("p (u j h) -> p u j h", j=T2, h=D),
                                        av.to_broadcast([P, tiles, T2, D]), ALU.mult).then_inc(e["used"], 1)
                    dve.wait_ge(e["used"], 8 * c + (4 * par + 4))
                    V.tensor_reduce(v3(raw[:, :]), prod[:, 0:CW].rearrange("p (u j h) -> p u h j", j=T2, h=D),
                                    AX.X, ALU.add).then_inc(e["preact"], 1)
                    dve.wait_ge(e["expo"], 2 * c + (par + 1))
                    own.did(V.tensor_scalar_add(basis[:, :], basis[:, :], 1.0))
                    own.settle()
                    own.did(V.reciprocal(basis[:, :], basis[:, :]))
                    own.settle()
                    V.scalar_tensor_tensor(raw[:, :], raw[:, :], NORM_MSG, basis[:, :], ALU.mult, ALU.mult)\
                        .then_inc(e["raw"], 1)

            def edge_phase(l):
                e = ed[l]
                for par in range(2):
                    stage(l, par, par * U).then_inc(e["staged"], 1)
                with dve.Fori(0, PAIRS) as c:
                    own.begin(c, STEPS[l])
                    for par in range(2):
                        col = (2 * c + par) * U
                        dve.wait_ge(gath[l][par], c * GATH + GATH)
                        V.tensor_copy(key[:, :], KEY[l][:, bass.ds(col, U)]).then_inc(e["key"], 1)
                        stage(l, par, col + AHEAD * U)
                        if l == 2:
                            fv = [v3(feat[:, s * 2 * P:s * 2 * P + U * D]) for s in range(2)]
                            for s in range(2):
                                own.did(V.tensor_tensor(fv[s], v3(rows[par][:, 0:U * D]),
                                                        gains[s][:, None, :].to_broadcast([P, U, D]), ALU.mult))
                            own.settle()
                            for s in range(2):
                                own.did(V.tensor_tensor(fv[s], fv[s], shifts[s][:, None, :].to_broadcast([P, U, D]),
                                                        ALU.add))
                            own.settle()
                            V.tensor_scalar(feat[:, :], feat[:, :], 0.0, None, ALU.max).then_inc(e["feat"], 1)
                        dve.wait_ge(e["keyT"], 2 * c + (par + 1))
                        V.tensor_tensor(v3(same[:, :], P), v3(psK[:, 0:CW], P), spread(key[:, :], P), ALU.is_equal)\
                            .then_inc(e["same"], 1)
                        messages(l, c, par, col)
                        if l < 2:
                            dve.wait_ge(e["same"], 2 * c + (par + 1))
                            if l == 1:
                                dve.wait_ge(e["raw"], 2 * c + (par + 1))
                            before, first = small[:, 0:U], small[:, U:2 * U]
                            own.did(V.tensor_tensor(v3(prod[:, 0:CW], P), v3(same[:, :], P),
                                                    lower[:, None, :].to_broadcast([P, U, P]), ALU.mult))
                            own.did(V.tensor_scalar(first, key[:, :], pad_row[:, :], None, ALU.subtract))
                            own.settle()
                            own.did(V.tensor_reduce(before, v3(prod[:, 0:CW], P), AX.X, ALU.add))
                            own.settle()
                            own.did(V.scalar_tensor_tensor(first, before, 0.0, first, ALU.is_equal, ALU.mult))
                            own.settle()
                            own.did(V.tensor_scalar(sidx[par][:, :], first, pad_row[:, :], None, ALU.add))
                            own.settle()
                            own.did(V.tensor_copy(TO[l][:, bass.ds(col, U)], sidx[par][:, :]))
                        else:
                            own.did(V.tensor_copy(sidx[par][:, :], TO[l][:, bass.ds(col, U)]))
                        dve.wait_ge(e["sum"], 2 * c + (par + 1))
                        V.tensor_copy(msgs[par][:, :], psM[:, 0:U * D]).then_inc(e["msg"], 1)
                        for s in range(2):
                            dve.wait_ge(scat[l][s], c * (2 * SCAT) + (FREE + par * SCAT))
                    if l == 2:
                        root(c)
                own.end(PAIRS)

            def root(c):
                w = RB * P
                hs, xs = h[:, bass.ds(c * w, w)], x[:, bass.ds(c * w, w)]
                for s in range(2):
                    r = rt[:, s * w:(s + 1) * w]
                    own.did(V.tensor_tensor(v3(r), v3(hs), gains[s][:, None, :].to_broadcast([P, RB * 8, D]), ALU.mult))
                    own.settle()
                    own.did(V.tensor_tensor(v3(r), v3(r), shifts[s][:, None, :].to_broadcast([P, RB * 8, D]), ALU.add))
                    own.settle()
                    V.tensor_scalar(r, r, 0.0, None, ALU.max).then_inc(rt_s["feat"], 1)
                own.did(V.tensor_tensor(v3(xs), v3(xs), bias16[:, None, :].to_broadcast([P, RB * 8, D]), ALU.add))
                own.settle()
                dve.wait_ge(rt_s["root"], c + 1)
                own.did(V.tensor_tensor(xs, xs, psK[:, 0:w], ALU.add))
                own.settle()

            for l in range(4):
                node_phase(l)
                edge_phase(l)
                if l == 1:
                    dve.wait_ge(w4_psum, 1)
                    for v in range(8):
                        k = V.tensor_scalar(W4[:, v * 256:(v + 1) * 256], psM[:, 0:256], rowmask[:, v:v + 1], NORM_LIN,
                                            ALU.mult, ALU.mult)
                    k.then_inc(w4_ready, 1)

            with dve.Fori(0, NCH) as c:
                own.begin(c, 4 * BLK + 2)
                xs, hs = x[:, bass.ds(c * CW, CW)], h[:, bass.ds(c * CW, CW)]
                dve.wait_ge(up["load"], 32 * c + 32)
                V.tensor_tensor(tC, tA[:, :], tB[:, :], ALU.add).then_inc(up["taken"], 1)
                own.did(V.tensor_tensor(xs, xs, hs, ALU.add))
                for m in range(4 * BLK):
                    dve.wait_ge(up["prod"], c * (4 * BLK) + (m + 1))
                    t = (feat, featT)[m % 2]
                    if m >= 2:
                        own.settle(but=1)
                    V.tensor_tensor(v3(t[:, :]), v3(psP[m % 2][:, :]),
                                    spread(h[:, bass.ds(c * CW + 32 * m, 32)]), ALU.mult).then_inc(up["used"], 1)
                    dve.wait_ge(up["used"], c * (4 * BLK) + (m + 1))
                    k = V.tensor_reduce(v3(tD[:, 32 * m:32 * m + 32]),
                                        t[:, :].rearrange("p (u i k) -> p u k i", i=D, k=D), AX.X, ALU.add)
                    if m < 4 * BLK - 1:
                        own.did(k)
                k.then_inc(up["preact"], 1)
                dve.wait_ge(up["expo"], c + 1)
                own.did(V.tensor_scalar_add(tC, tC, 1.0))
                own.settle()
                own.did(V.reciprocal(tC, tC))
                own.settle()
                V.scalar_tensor_tensor(tC, tD, NORM_UPD, tC, ALU.mult, ALU.mult).then_inc(up["silu"], 1)
                dve.wait_ge(up["update"], c + 1)
                V.scalar_tensor_tensor(xs, psK[:, 0:CW], NORM_LIN, xs, ALU.mult, ALU.add).then_inc(up["done"], 1)
            own.end(NCH)


_INS = ["x", "src", "dst", "edge_attr_2", "edge_attr_8", "edge_attr_8_reversed", "edge_weight", "node_vec1", "L0_gnn_weight",
        "L0_gnn_self_loop_weight", "L1_gnn_weight", "L2_gnn_ln_g_n", "L2_gnn_ln_b_n", "L2_gnn_We_n",
        "L2_gnn_be_n", "L2_gnn_Wr_n", "L2_gnn_b_n", "L2_gnn_ln_g_r", "L2_gnn_ln_b_r", "L2_gnn_We_r",
        "L2_gnn_be_r", "L2_gnn_Wr_r", "L2_gnn_b_r", "L3_gnn_W_msg_tp", "L3_gnn_W_msg_lin",
        "L3_gnn_W_upd_tp", "L3_gnn_W_upd_lin"]


def kernel(**inputs):
    import numpy as _np
    import concourse.bacc as _bacc
    from concourse import mybir as _mybir
    from concourse.bass_utils import run_bass_kernel_spmd as _run

    nc = _bacc.Bacc("TRN2", target_bir_lowering=False, num_devices=1)
    inputs["edge_attr_8_reversed"] = _np.ascontiguousarray(_np.asarray(inputs["edge_attr_8"])[::-1])
    arrays, args = {}, []
    for name in _INS:
        a = _np.ascontiguousarray(inputs[name])
        a = a.reshape(a.shape or (1,))
        arrays[f"in_{name}_dram"] = a
        args.append(nc.dram_tensor(f"in_{name}_dram", a.shape, _mybir.dt.from_np(a.dtype), kind="ExternalInput").ap())
    out = nc.dram_tensor("out_0_dram", (N, D), _mybir.dt.float32, kind="ExternalOutput").ap()
    build_gnn(nc, *args, out)
    r = _run(nc, [arrays], core_ids=[0])
    return r.results[0]["out_0_dram"]
```

```python
import concourse.bass as bass
from concourse import mybir
from contextlib import ExitStack


P = 128
N, E, D = 100000, 50000, 16
COLS = 784
NPAD = P * COLS
ROWS = NPAD + P
CH = 112
NCH = COLS // CH
CW = CH * D
RB = 7
BLK = CW // P
FULL = N // COLS
LAST = N - FULL * COLS
WIDE = FULL // 16 * 16
ZW = 448
U = 14
TILES = 392
GROUPS = TILES // U
PAIRS = GROUPS // 2
ET = E // P
REST = E - ET * P
AHEAD = 2
ICOLS = TILES + AHEAD * U
T2 = 8
A9 = T2 + 1
HALF = 8
EPS = 1e-5


class Steps:

    def __init__(self, eng, sem):
        self.eng, self.sem, self.base, self.turn, self.per, self.k = eng, sem, 0, 0, 0, 0

    def begin(self, turn, per):
        self.turn, self.per, self.k = turn, per, 0

    def end(self, turns):
        assert self.k == self.per, (self.k, self.per)
        self.base += self.per * turns
        self.begin(0, 0)

    def did(self, instruction):
        self.k += 1
        instruction.then_inc(self.sem, 1)

    def settle(self, but=0):
        self.eng.wait_ge(self.sem, self.turn * self.per + (self.base + self.k - but))


def build_gnn(nc, x_in, src_in, dst_in, attr2_in, attr8_in, attr8_rev_in, ew_in, vec1_in, w0_in, slw_in, w1_in,
              g_n_in, b_n_in, We_n_in, be_n_in, Wr_n_in, bias_n_in,
              g_r_in, b_r_in, We_r_in, be_r_in, Wr_r_in, bias_r_in,
              Wmsg_in, Wmlin_in, Wupd_in, Wulin_in, out):
    f32, i32 = mybir.dt.float32, mybir.dt.int32
    ALU, ACT, AX = mybir.AluOpType, mybir.ActivationFunctionType, mybir.AxisListType
    NORM_MSG = float((D * T2) ** -0.5)
    NORM_UPD = float((D * D) ** -0.5)
    NORM_LIN = float(D ** -0.5)

    ctx = ExitStack()
    with ctx:
        def sb(name, shape, dt=f32):
            return ctx.enter_context(nc.sbuf_tensor(name, shape, dt))

        def sem(name):
            return ctx.enter_context(nc.semaphore(name))

        table = nc.dram_tensor("table", (ROWS, D), f32)
        accum = [[nc.dram_tensor(f"accum{l}_{s}", (ROWS, D), f32) for s in range(2)]
                 for l in range(4)]

        x = sb("x", [P, COLS * D])
        h = sb("h", [P, COLS * D])
        src = sb("src", [P, ICOLS], i32)
        dst = sb("dst", [P, ICOLS], i32)
        to_src = sb("to_src", [P, TILES], i32)
        to_dst = sb("to_dst", [P, TILES], i32)
        ew = sb("ew", [P, TILES])
        attr2 = sb("attr2", [P, TILES * 2])
        attr8 = sb("attr8", [P, TILES * T2])
        rev8 = [sb(f"rev8_{p}", [P, U * T2]) for p in range(2)]
        gidx = [sb(f"gidx{p}", [P, U], i32) for p in range(2)]
        sidx = [sb(f"sidx{p}", [P, U], i32) for p in range(2)]
        rows = [sb(f"rows{p}", [P, 2 * P]) for p in range(2)]
        msgs = [sb(f"msgs{p}", [P, U * D]) for p in range(2)]
        key = sb("key", [P, U])
        same = sb("same", [P, CW])
        tB = sb("tB", [P, CW])
        prod = sb("prod", [P, 2 * CW])
        raw = sb("raw", [P, U * D])
        small = sb("small", [P, 8 * CH])
        basis = sb("basis", [P, U * D])
        feat = sb("feat", [P, 4 * P])
        featT = sb("featT", [P, 4 * P])
        ident = sb("ident", [P, P])
        lower = sb("lower", [P, P])
        rowmask = sb("rowmask", [P, 8])
        pad_row = sb("pad_row", [P, 1])
        eps = sb("eps", [P, 1])
        w0 = sb("w0", [P, D])
        slw1 = sb("slw1", [P, 1])
        gains = [sb(f"gain{s}", [P, D]) for s in range(2)]
        shifts = [sb(f"shift{s}", [P, D]) for s in range(2)]
        bias16 = sb("bias16", [P, D])
        W1 = sb("W1", [P, 4 * 512])
        W2 = [sb(f"W2_{s}", [P, 2 * 288]) for s in range(2)]
        W3 = sb("W3", [P, 2 * 512])
        Wroot = [sb(f"Wroot{s}", [P, P]) for s in range(2)]
        W4 = W1
        Wfin = sb("Wfin", [P, P])
        mlinT = sb("mlinT", [D, P])
        upd = sb("upd", [D, D * D])

        zeros = sb("zeros", [P, ZW])
        rt = sb("rt", [P, 2 * CW])

        psK = ctx.enter_context(nc.psum_tensor("psK", [P, 2048], f32))
        psX = ctx.enter_context(nc.psum_tensor("psX", [P, 2048], f32))
        psT = psX[:, 0:512]
        psP = [psX[:, 512:1024], psX[:, 1024:1536]]
        psM = psX[:, 1536:2048]
        psQ = [psX[:, 0:1024], psX[:, 1024:2048]]

        loaded = sem("loaded")
        cleared = sem("cleared")
        masks = sem("masks")
        w4_ready = sem("w4_ready")
        w4_psum = sem("w4_psum")
        zeroed = [sem(f"zeroed{l}") for l in range(4)]
        stored = sem("stored")
        names = ("staged",
                 "key",
                 "keyT",
                 "same",
                 "feat",
                 "bandT",
                 "bandS",
                 "prod",
                 "used",
                 "preact",
                 "raw",
                 "sum",
                 "msg")
        lacks = [("feat", "bandT", "bandS", "prod", "used", "preact"), ("feat", "preact"), ("preact",), ("feat",)]
        ed = [{n: sem(f"e{l}_{n}") for n in names if n not in lacks[l]} for l in range(4)]
        pool_go = sem("pool_go")
        rev_in = [sem(f"rev_in{p}") for p in range(2)]
        rev_rest = sem("rev_rest")
        gath = [[sem(f"e{l}_gath{p}") for p in range(2)] for l in range(4)]
        scat = [[sem(f"e{l}_scat{s}") for s in range(2)] for l in range(4)]
        nnames = ("loadA", "loadB",
                  "takenA", "takenB",
                  "relu",
                  "update",
                  "center", "center2",
                  "square", "square2",
                  "varsum", "varsum2",
                  "sdev", "sdev2",
                  "norm", "norm2",
                  "store")
        lacks = [nnames[0:6], (), ("relu", "update"), ("relu", "update")]
        nd = [{n: sem(f"n{l}_{n}") for n in nnames if (l == 2 or n[-1] != "2") and n not in lacks[l]}
              for l in range(4)]
        unames = ("loadA", "loadB",
                  "total",
                  "resid",
                  "totalT", "totalS",
                  "prod", "used",
                  "half",
                  "preact", "silu",
                  "siluT", "siluS",
                  "update",
                  "done")
        up = {n: sem(f"u_{n}") for n in unames}
        rnames = ("feat", "bandT", "bandS", "root")
        rt_s = {n: sem(f"r_{n}") for n in rnames}
        dve_go = sem("dve_go")
        dve_step = sem("dve_step")

        def v3(ap, f=D):
            return ap.rearrange("p (u f) -> p u f", f=f)

        def node_rows(t, w=D):
            return t.ap()[0:NPAD, :].rearrange("(p c) f -> p (c f)", p=P)

        mean, var, sdev, inv, mean2, var2, sdev2, inv2 = [small[:, i * CH:(i + 1) * CH] for i in range(8)]
        tA, tC, tD = same, prod[:, 0:CW], prod[:, CW:2 * CW]
        load_incs = [0]
        MASKS = 9
        own_peeled = [(1, 1), (2, 1), (4, 4), (1, 1)]
        own_turn = [2, 3, 4, 2]
        STEPS = [14, 26, 16, 2]
        LOADS = 16 * 102
        CLEARED = 22

        QUADS = CH // 4
        wide = [attr8[:, i * 1024:(i + 1) * 1024] for i in range(2)]
        halves = [attr8[:, 2048 + i * 512:2048 + (i + 1) * 512] for i in range(2)]

        def products(q):
            return (wide[q % 2].rearrange("p (u i k) -> p u i k", i=D, k=D),
                    halves[q % 2].rearrange("p (u i k) -> p u i k", i=D // 2, k=D))

        block = ctx.enter_context(nc.Block())

        GATHER = [src, dst, src, dst]
        KEY = [dst, src, dst, src]
        TO = [to_dst, to_src, to_dst, to_src]
        GATH = 16 * U
        SCAT = 16 * U // 2
        FREE = 16

        @block.sync
        def _(sp):
            def load(o, i):
                load_incs[0] += 16
                sp.dma_start(o, i).then_inc(loaded, 16)

            sp.wait_ge(cleared, CLEARED)
            sp.wait_ge(masks, MASKS)
            for a, b in ((0, WIDE), (WIDE, FULL)):
                load(x[a:b, :], x_in[a * COLS:b * COLS, :].rearrange("(p c) f -> p (c f)", c=COLS))
            load(x[FULL:FULL + 1, 0:LAST * D],
                 x_in[FULL * COLS:N, :].rearrange("(p c) f -> p (c f)", p=1))
            with nc.allow_non_contiguous_dma(reason="the last column of edges and small weights"):
                for t, a, w in ((src, src_in, 1), (dst, dst_in, 1), (ew, ew_in, 1)):
                    load(t[:, 0:ET], a[0:ET * P].rearrange("(p c) -> p c", p=P))
                    load(t[0:REST, ET:ET + 1], a[ET * P:E].rearrange("(p c) -> p c", c=1))
                a2, a8 = v3(attr2[:, :], 2), v3(attr8[:, :], T2)
                load(a2[:, 0:ET, :], attr2_in[0:ET * P, :].rearrange("(p c) f -> p c f", p=P))
                load(a2[0:REST, ET, :], attr2_in[ET * P:E, :])
                load(a8[:, 0:ET, :], attr8_in[0:ET * P, :].rearrange("(p c) f -> p c f", p=P))
                load(a8[0:REST, ET, :], attr8_in[ET * P:E, :])
                load(w0[:, :], w0_in[None, :].to_broadcast([P, D]))
                load(slw1[:, :], slw_in[None, :].to_broadcast([P, 1]))
                for s, (g, b) in enumerate(((g_n_in, b_n_in), (g_r_in, b_r_in))):
                    load(gains[s][:, :], g[None, :].to_broadcast([P, D]))
                    load(shifts[s][:, :], b[None, :].to_broadcast([P, D]))
                load(bias16[:, 0:HALF], bias_n_in[None, :].to_broadcast([P, HALF]))
                load(bias16[:, HALF:D], bias_r_in[None, :].to_broadcast([P, HALF]))
                w1v = w1_in.rearrange("a b i o -> i (a b) o")
                w3v = Wmsg_in.rearrange("i j h -> i (j h)")
                for v in range(8):
                    band = slice(D * v, D * v + D)
                    c1 = (v // 2) * 512 + (v % 2) * 256
                    load(v3(W1[:, :])[band, c1 // D:c1 // D + D, :], w1v)
                    c3 = v * P
                    load(W3[band, c3:c3 + P], w3v)
                    for s, (We, be, Wr) in enumerate(((We_n_in, be_n_in, Wr_n_in),
                                                      (We_r_in, be_r_in, Wr_r_in))):
                        c2 = v * A9
                        w2 = v3(W2[s][:, :], HALF)
                        load(w2[band, c2:c2 + T2, :], We.rearrange("t (i o) -> i t o", o=HALF))
                        load(w2[band, c2 + T2, :], be.rearrange("(i o) -> i o", o=HALF))
                        load(Wroot[s][band, v * D + s * HALF:v * D + (s + 1) * HALF], Wr)
                    load(Wfin[band, v * D:v * D + D], Wulin_in)
                    load(mlinT[:, band], Wmlin_in.rearrange("q h -> h q"))
                load(v3(upd[:, :]), Wupd_in.rearrange("i h k -> h i k"))

            assert load_incs[0] == LOADS, load_incs

            def zero(l, start, cols, width):
                for s in range(2):
                    sp.dma_start(accum[l][s].ap()[0:NPAD, :].rearrange("(p c) f -> p (c f)", p=P)
                                 [:, bass.ds(start * D, cols * D)].rearrange("p (k w) -> p k w", w=width),
                                 zeros[:, None, 0:width].to_broadcast([P, cols * D // width, width]))\
                        .then_inc(zeroed[l], 16)

            sp.dma_start(table.ap()[NPAD:ROWS, :], zeros[:, 0:D]).then_inc(zeroed[0], 16)
            zero(0, 0, COLS, ZW)
            for l in range(4):
                if l == 2:
                    rev = attr8_rev_in[0:ET * P, :].rearrange("(p c) f -> p (c f)", p=P)

                    def reverse(par, col, cols=U):
                        sp.dma_start(rev8[par][:, 0:cols * T2], rev[:, bass.ds(col * T2, cols * T2)])\
                            .then_inc(rev_in[par], 16)

                    reverse(0, 0)
                    reverse(1, U)
                piece = COLS // PAIRS
                if l in (0, 1):
                    with sp.Fori(0, PAIRS) as c:
                        sp.wait_ge(ed[l]["msg"], 2 * c + 1)
                        zero(l + 1, c * piece, piece, ZW)
                if l == 2:
                    zero(3, 0, piece, ZW)
                    with sp.Fori(1, PAIRS - 1) as c:
                        for par in range(2):
                            sp.wait_ge(ed[l]["msg"], 2 * c + (par - 1))
                            reverse(par, (2 * c + par) * U)
                        zero(3, c * piece, piece, ZW)
                    sp.wait_ge(ed[l]["msg"], GROUPS - 3)
                    reverse(0, (GROUPS - 2) * U)
                    sp.wait_ge(ed[l]["msg"], GROUPS - 2)
                    left = ET - (GROUPS - 1) * U
                    sp.dma_start(rev8[1][0:REST, left * T2:(left + 1) * T2], attr8_rev_in[ET * P:E, :])\
                        .then_inc(rev_rest, 16)
                    sp.wait_ge(rev_rest, 16)
                    reverse(1, (GROUPS - 1) * U, left)
                    zero(3, (PAIRS - 1) * piece, piece, ZW)
                for s in range(2):
                    sp.wait_ge(scat[l][s], FREE + SCAT * GROUPS)
                sp.wait_ge(ed[l]["same"], GROUPS + 1)
                n = nd[l + 1] if l < 3 else up
                freed = (n["takenA"], n["takenB"]) if l < 3 else (n["totalT"], n["total"])
                arrived = (n["loadA"], n["loadB"])

                def fetch(s, c):
                    sp.dma_start((tA, tB)[s][:, :], node_rows(accum[l][s])[:, bass.ds(c * CW, CW)])\
                        .then_inc(arrived[s], 16)

                fetch(0, 0)
                fetch(1, 0)
                with sp.Fori(1, NCH) as c:
                    for s in range(2):
                        sp.wait_ge(freed[s], c)
                        fetch(s, c)

        @block.gpsimd
        def _(pool):
            pool.memset(ident[:, :], 0.0).then_inc(masks, 1)
            pool.memset(lower[:, :], 1.0).then_inc(masks, 1)
            pool.memset(rowmask[:, :], 1.0).then_inc(masks, 1)
            for t in (src, dst):
                pool.iota(t[:, ET:ICOLS], pattern=[[0, ICOLS - ET]], base=NPAD, channel_multiplier=1)\
                    .then_inc(masks, 1)
            pool.wait_ge(masks, 3)
            pool.affine_select(out=ident[:, :], in_=ident[:, :], compare_op=ALU.not_equal, fill=1.0, base=0,
                               pattern=[[-1, P]], channel_multiplier=1).then_inc(masks, 1)
            pool.affine_select(out=lower[:, :], in_=lower[:, :], compare_op=ALU.is_gt, fill=0.0, base=0,
                               pattern=[[-1, P]], channel_multiplier=1).then_inc(masks, 1)
            pool.affine_select(out=rowmask[:, :], in_=rowmask[:, :], compare_op=ALU.is_ge, fill=0.0, base=0,
                               pattern=[[-D, 8]], channel_multiplier=1).then_inc(masks, 1)
            pool.wait_ge(masks, MASKS - 1)
            pool.affine_select(out=rowmask[:, :], in_=rowmask[:, :], compare_op=ALU.is_ge, fill=0.0, base=D - 1,
                               pattern=[[D, 8]], channel_multiplier=-1).then_inc(masks, 1)

            for l in range(4):
                e = ed[l]

                def gather(par, u):
                    pool.indirect_dma_start(
                        out=rows[par][:, u * D:(u + 1) * D], out_offset=None, in_=table.ap(),
                        in_offset=bass.IndirectOffsetOnAxis(ap=gidx[par][:, u:u + 1], axis=0))\
                        .then_inc(gath[l][par], 16)

                def scatter(par, turn, and_gather):
                    for u in range(U):
                        pool.wait_ge(scat[l][u % 2], turn * (2 * SCAT) + (FREE + par * SCAT + 16 * (u // 2)))
                        pool.sem_inc(pool_go, 1)
                        pool.indirect_dma_start(
                            out=accum[l][u % 2].ap(),
                            out_offset=bass.IndirectOffsetOnAxis(ap=sidx[par][:, u:u + 1], axis=0),
                            in_=msgs[par][:, u * D:(u + 1) * D], in_offset=None, compute_op=ALU.add)\
                            .then_inc(scat[l][u % 2], 16)
                        if and_gather:
                            gather(par, u)

                pool.wait_ge(cleared, CLEARED)
                for s in range(2):
                    pool.dma_start(accum[l][s].ap()[NPAD:ROWS, :], zeros[:, 0:D]).then_inc(scat[l][s], FREE)
                if l:
                    n = nd[l]
                    with pool.Fori(0, NCH) as c:
                        xs = x[:, bass.ds(c * CW, CW)]
                        pool.wait_ge(n["loadA"], 16 * c + 16)
                        pool.sem_inc(pool_go, 1)
                        if l == 1:
                            pool.wait_ge(n["loadB"], 16 * c + 16)
                            nc.gpsimd.tensor_tensor(tA[:, :], tA[:, :], tB[:, :], ALU.add)\
                                .then_inc(n["takenB"], 1)
                        else:
                            nc.gpsimd.tensor_tensor(xs, xs, tA[:, :], ALU.add).then_inc(n["takenA"], 1)
                            pool.wait_ge(n["loadB"], 16 * c + 16)
                            pool.sem_inc(pool_go, 1)
                            pool.wait_ge(n["takenA"], c + 1)
                            pool.sem_inc(pool_go, 1)
                            nc.gpsimd.tensor_tensor(xs, xs, tB[:, :], ALU.add).then_inc(n["takenB"], 1)
                pool.wait_ge(nd[l]["store"], 16 * NCH)
                pool.wait_ge(e["staged"], 2)
                if l == 0:
                    pool.wait_ge(zeroed[0], 16 * 3)
                pool.sem_inc(pool_go, 1)
                for par in range(2):
                    for u in range(U):
                        gather(par, u)
                if l:
                    pool.wait_ge(zeroed[l], 16 * 2)
                with pool.Fori(0, PAIRS - 1) as c:
                    for par in range(2):
                        pool.wait_ge(e["msg"], 2 * c + (par + 1))
                        pool.sem_inc(pool_go, 1)
                        scatter(par, c, True)
                for par in range(2):
                    pool.wait_ge(e["msg"], 2 * (PAIRS - 1) + par + 1)
                    scatter(par, PAIRS - 1, False)

            def total():
                nc.gpsimd.tensor_tensor(tA[:, :], tA[:, :], tB[:, :], ALU.add).then_inc(up["total"], 1)

            def update(c, last):
                xs = x[:, bass.ds(c * CW, CW)]
                nc.gpsimd.tensor_tensor(xs, xs, h[:, bass.ds(c * CW, CW)], ALU.add).then_inc(up["resid"], 1)
                for q in range(QUADS):
                    if q == QUADS // 2 and not last:
                        pool.wait_ge(up["loadA"], 16 * c + 32)
                        pool.sem_inc(pool_go, 1)
                        pool.wait_ge(up["loadB"], 16 * c + 32)
                        total()
                    w, hf = products(q)
                    pool.wait_ge(up["used"], c * QUADS + (q + 1))
                    nc.gpsimd.tensor_tensor(hf, w[:, :, 0:8, :], w[:, :, 8:16, :], ALU.add).then_inc(up["half"], 1)

            pool.wait_ge(up["loadA"], 16)
            pool.sem_inc(pool_go, 1)
            pool.wait_ge(up["loadB"], 16)
            total()
            with pool.Fori(0, NCH - 1) as c:
                update(c, False)
            update(NCH - 1, True)

        @block.tensor
        def _(pe):
            pe.wait_ge(masks, MASKS)
            pe.wait_ge(loaded, LOADS)
            def root_term(c):
                for s in range(2):
                    pe.wait_ge(rt_s["feat"], 2 * c + (s + 1))
                    if s:
                        pe.wait_ge(rt_s["bandS"], 2 * c + s)
                    for b in range(RB):
                        k = nc.tensor.transpose(psK[:, b * P:(b + 1) * P],
                                                rt[:, (s * RB + b) * P:(s * RB + b + 1) * P], ident[:, :])
                    k.then_inc(rt_s["bandT"], 1)
                pe.wait_ge(rt_s["bandS"], 2 * c + 2)
                for b in range(RB):
                    for s in range(2):
                        k = nc.tensor.matmul(psK[:, b * P:(b + 1) * P],
                                             rt[:, ((2 + s) * RB + b) * P:((2 + s) * RB + b + 1) * P],
                                             Wroot[s][:, :], start=s == 0, stop=s == 1)
                k.then_inc(rt_s["root"], 1)


            for l in range(4):
                e = ed[l]

                def key_rows(g):
                    pe.wait_ge(e["key"], g + 1)
                    for u in range(U):
                        k = nc.tensor.transpose(psK[:, u * P:(u + 1) * P],
                                                key[:, u:u + 1].to_broadcast([P, P]), ident[:, :])
                    k.then_inc(e["keyT"], 1)

                key_rows(0)
                with pe.Fori(0, PAIRS) as c:
                    for par in range(2):
                        if l:
                            if l == 2:
                                pe.wait_ge(e["feat"], 2 * c + (par + 1))
                                bands = [feat[:, b * P:(b + 1) * P] for b in range(4)]
                            else:
                                pe.wait_ge(gath[l][par], c * GATH + GATH)
                                bands = [rows[par][:, b * P:(b + 1) * P] for b in range(2)]
                            for b, band in enumerate(bands):
                                k = nc.tensor.transpose(psT[:, b * P:(b + 1) * P], band, ident[:, :])
                            k.then_inc(e["bandT"], 1)
                            pe.wait_ge(e["bandS"], 2 * c + (par + 1))
                            if l == 1:
                                parts = [(m // 4, W1[:, (m % 4) * 512:(m % 4 + 1) * 512]) for m in range(7)]
                            elif l == 3:
                                parts = [(m // 2, W3[:, (m % 2) * 512:(m % 2 + 1) * 512]) for m in range(4)]
                            else:
                                parts = [(2 * s + m // 2, W2[s][:, (m % 2) * 288:(m % 2 + 1) * 288])
                                         for s in range(2) for m in range(4)]
                            n = len(parts)
                            for m, (b, w) in enumerate(parts):
                                if m >= 2:
                                    pe.wait_ge(e["used"], c * (2 * n) + (par * n + m - 1))
                                nc.tensor.matmul(psP[m % 2][:, 0:w.shape[1]], featT[:, b * P:(b + 1) * P], w,
                                                 start=True, stop=True).then_inc(e["prod"], 1)
                        pe.wait_ge(e["same"], 2 * c + (par + 1))
                        pe.wait_ge(e["raw"], 2 * c + (par + 1))
                        for u in range(U):
                            k = nc.tensor.matmul(psM[:, u * D:(u + 1) * D], same[:, u * P:(u + 1) * P],
                                                 raw[:, u * D:(u + 1) * D], start=True, stop=True)
                        k.then_inc(e["sum"], 1)
                        if l == 2 and par:
                            root_term(c)
                        key_rows(2 * c + (par + 1))
                if l == 1:
                    pe.wait_ge(e["msg"], GROUPS)
                    nc.tensor.matmul(psM[:, 0:256], mlinT[:, :], upd[:, :], start=True, stop=True)\
                        .then_inc(w4_psum, 1)
                    pe.wait_ge(w4_ready, 1)

            def step_sums(c):
                pe.wait_ge(up["total"], c + 1)
                for b in range(BLK):
                    k = nc.tensor.transpose(psK[:, b * P:(b + 1) * P], tA[:, b * P:(b + 1) * P], ident[:, :])
                k.then_inc(up["totalT"], 1)
                pe.wait_ge(up["totalS"], c + 1)

            def step_products(c, first, quads):
                for q in quads:
                    if not first or q >= 2:
                        pe.wait_ge(up["used"], c * QUADS + (q - 1))
                    for j in range(2):
                        b, m = q // 2, 2 * (q % 2) + j
                        k = nc.tensor.matmul(psQ[q % 2][:, j * 512:(j + 1) * 512], rt[:, b * P:(b + 1) * P],
                                             W4[:, m * 512:(m + 1) * 512], start=True, stop=True)
                    k.then_inc(up["prod"], 1)

            def step_update(c):
                pe.wait_ge(up["silu"], c + 1)
                for b in range(BLK):
                    k = nc.tensor.transpose(psK[:, b * P:(b + 1) * P], tC[:, b * P:(b + 1) * P], ident[:, :])
                k.then_inc(up["siluT"], 1)
                pe.wait_ge(up["siluS"], c + 1)
                for b in range(BLK):
                    k = nc.tensor.matmul(psK[:, b * P:(b + 1) * P], rt[:, CW + b * P:CW + (b + 1) * P], Wfin[:, :],
                                         start=True, stop=True)
                k.then_inc(up["update"], 1)

            EARLY = 10
            step_sums(0)
            step_products(0, True, range(QUADS))
            with pe.Fori(1, NCH) as c:
                step_sums(c)
                step_products(c, False, range(EARLY))
                step_update(c - 1)
                step_products(c, False, range(EARLY, QUADS))
                pe.wait_ge(up["done"], c)
            step_update(NCH - 1)

        @block.scalar
        def _(act):
            def square(n, c, which=""):
                act.wait_ge(n["center" + which], c + 1)
                nc.scalar.activation(tC if which else tD, h[:, bass.ds(c * CW, CW)], ACT.Square)\
                    .then_inc(n["square" + which], 1)

            def root(n, c, which=""):
                act.wait_ge(n["varsum" + which], c + 1)
                nc.scalar.activation(sdev2 if which else sdev, var2 if which else var, ACT.Sqrt, bias=eps[:, :],
                                     scale=1.0 / D).then_inc(n["sdev" + which], 1)

            def relu(n, c):
                act.wait_ge(n["update"], c + 1)
                nc.scalar.activation(tC, tC, ACT.Relu).then_inc(n["relu"], 1)

            def store(n, c, which=""):
                act.wait_ge(n["norm" + which], c + 1)
                act.dma_start(node_rows(table)[:, bass.ds(c * CW, CW)], h[:, bass.ds(c * CW, CW)])\
                    .then_inc(n["store"], 16)

            for d in range(4):
                n, e = nd[d], ed[d]
                if d == 2:
                    square(n, 0)
                    root(n, 0)
                    square(n, 1)
                    square(n, 0, "2")
                    with act.Fori(2, NCH) as c:
                        root(n, c - 1)
                        square(n, c)
                        root(n, c - 2, "2")
                        square(n, c - 1, "2")
                        store(n, c - 2, "2")
                    root(n, NCH - 1)
                    root(n, NCH - 2, "2")
                    square(n, NCH - 1, "2")
                    store(n, NCH - 2, "2")
                    root(n, NCH - 1, "2")
                    store(n, NCH - 1, "2")
                else:
                    if d == 1:
                        relu(n, 0)
                    square(n, 0)
                    with act.Fori(1, NCH) as c:
                        if d == 1:
                            relu(n, c)
                        root(n, c - 1)
                        square(n, c)
                        store(n, c - 1)
                    root(n, NCH - 1)
                    store(n, NCH - 1)
                if d:
                    with act.Fori(0, PAIRS) as c:
                        for par in range(2):
                            w = 4 * P if d == 2 else 2 * P
                            act.wait_ge(e["bandT"], 2 * c + (par + 1))
                            nc.scalar.activation(featT[:, 0:w], psT[:, 0:w], ACT.Copy).then_inc(e["bandS"], 1)
                            if d == 3:
                                act.wait_ge(e["preact"], 2 * c + (par + 1))
                                nc.scalar.activation(raw[:, :], basis[:, :], ACT.Silu, scale=NORM_MSG)\
                                    .then_inc(e["raw"], 1)
                        if d == 2:
                            for s in range(2):
                                act.wait_ge(rt_s["bandT"], 2 * c + (s + 1))
                                nc.scalar.activation(rt[:, (2 + s) * RB * P:(3 + s) * RB * P], psK[:, 0:RB * P],
                                                     ACT.Copy).then_inc(rt_s["bandS"], 1)

            def copy_sums(c):
                act.wait_ge(up["totalT"], c + 1)
                nc.scalar.activation(rt[:, 0:CW], psK[:, 0:CW], ACT.Copy).then_inc(up["totalS"], 1)

            def finish(c):
                act.wait_ge(up["preact"], c + 1)
                nc.scalar.activation(tC, tD, ACT.Silu, scale=NORM_UPD).then_inc(up["silu"], 1)
                act.wait_ge(up["siluT"], c + 1)
                nc.scalar.activation(rt[:, CW:2 * CW], psK[:, 0:CW], ACT.Copy).then_inc(up["siluS"], 1)
                act.wait_ge(up["done"], c + 1)
                for a, b in ((0, WIDE), (WIDE, FULL)):
                    act.dma_start(out[a * COLS:b * COLS, :].rearrange("(p c) f -> p (c f)", c=COLS)
                                  [:, bass.ds(c * CW, CW)], x[a:b, bass.ds(c * CW, CW)]).then_inc(stored, 16)

            copy_sums(0)
            with act.Fori(1, NCH) as c:
                copy_sums(c)
                finish(c - 1)
            finish(NCH - 1)
            act.dma_start(out[FULL * COLS:N, :].rearrange("(p c) f -> p (c f)", p=1),
                          x[FULL:FULL + 1, 0:LAST * D]).then_inc(stored, 16)
            act.wait_ge(stored, 16 * (2 * NCH + 1))

        @block.vector
        def _(dve):
            V = nc.vector
            own = Steps(dve, dve_step)

            def clear(t, value=0.0):
                V.memset(t, value).then_inc(cleared, 1)

            clear(zeros[:, :])
            clear(x[96:P, LAST * D:])
            clear(ew[:, ET:])
            clear(attr2[:, 2 * ET:])
            clear(attr8[:, T2 * ET:])
            clear(feat[:, :])
            for par in range(2):
                clear(rows[par][:, :])
                clear(rev8[par][:, :])
            for t in (W1, W2[0], W2[1], W3, Wroot[0], Wroot[1], Wfin):
                clear(t[:, :])
            clear(eps[:, :], EPS)
            clear(key[:, :])
            clear(raw[:, :])
            clear(small[:, :])
            clear(msgs[0][:, :])

            dve.wait_ge(loaded, LOADS)
            own.begin(0, 2)
            own.did(V.tensor_copy(pad_row[:, :], dst[:, ICOLS - 1:ICOLS]))
            own.did(V.tensor_scalar_add(slw1[:, :], slw1[:, :], 1.0))
            own.settle()
            own.end(1)

            def spread(ap, f=D):
                return ap[:, :, None].to_broadcast([P, ap.shape[1], f])


            def part_mean(feats, m):
                dve.sem_inc(dve_go, 1)
                own.did(V.tensor_reduce(m, v3(feats), AX.X, ALU.add))

            def part_center(feats, hs, m, done):
                V.scalar_tensor_tensor(v3(hs), spread(m), -1.0 / D, v3(feats), ALU.mult, ALU.add).then_inc(done, 1)

            def part_var(n, c, which, squares, v):
                dve.wait_ge(n["square" + which], c + 1)
                V.tensor_reduce(v, v3(squares), AX.X, ALU.add).then_inc(n["varsum" + which], 1)

            def part_scale(n, c, which, hs, sd, i):
                dve.wait_ge(n["sdev" + which], c + 1)
                own.did(V.reciprocal(i, sd))
                own.settle()
                if which:
                    V.tensor_tensor(v3(hs), v3(hs), spread(i), ALU.mult).then_inc(n["norm2"], 1)
                else:
                    V.scalar_tensor_tensor(v3(hs), v3(hs), 0.0, spread(i), ALU.max, ALU.mult).then_inc(n["norm"], 1)

            def step_of(t, c):
                return t[:, bass.ds(c * CW, CW)]

            def node_phase(d):
                n = nd[d]

                def enter(c):
                    if d == 1:
                        dve.wait_ge(n["takenB"], c + 1)
                        V.scalar_tensor_tensor(tC, step_of(h, c), slw1[:, :], tA[:, :], ALU.mult, ALU.add)\
                            .then_inc(n["update"], 1)
                    elif d:
                        dve.wait_ge(n["takenB"], c + 1)

                def head(c, turn):
                    if d == 1:
                        dve.wait_ge(n["relu"], c + 1)
                        own.did(V.scalar_tensor_tensor(step_of(x, c), tC, 1.0, step_of(x, c), ALU.min, ALU.add))
                        own.settle()
                        dve.sem_inc(n["takenA"], 1)
                    if turn is not None:
                        dve.wait_ge(n["center"], c)
                    part_mean(step_of(x, c), mean)
                    own.settle()

                def second(c, first, last):
                    hs = None if last else step_of(h, c)
                    if not last:
                        dve.wait_ge(n["norm"], c + 1)
                        if not first:
                            dve.sem_inc(dve_go, 1)
                            dve.wait_ge(n["center2"], c)
                        part_mean(hs, mean2)
                    if not first:
                        part_var(n, c - 1, "2", tC, var2)
                    if not last:
                        own.settle()
                        part_center(hs, hs, mean2, n["center2"])
                    if not first:
                        part_scale(n, c - 1, "2", step_of(h, c - 1), sdev2, inv2)

                def body(c, turn, edge):
                    enter(c)
                    head(c, turn)
                    part_var(n, c - 1, "", tD, var)
                    part_center(step_of(x, c), step_of(h, c), mean, n["center"])
                    part_scale(n, c - 1, "", step_of(h, c - 1), sdev, inv)
                    if d == 2:
                        second(c - 1, edge, False)

                own.begin(0, own_peeled[d][0])
                enter(0)
                head(0, None)
                part_center(step_of(x, 0), step_of(h, 0), mean, n["center"])
                start = 1
                if d == 2:
                    body(1, 0, True)
                    start = 2
                own.end(1)
                with dve.Fori(start, NCH) as c:
                    own.begin(c - start, own_turn[d])
                    body(c, c, False)
                own.end(NCH - start)
                own.begin(0, own_peeled[d][1])
                part_var(n, NCH - 1, "", tD, var)
                part_scale(n, NCH - 1, "", step_of(h, NCH - 1), sdev, inv)
                if d == 2:
                    second(NCH - 1, False, False)
                    second(NCH, False, True)
                own.end(1)
                done = "norm2" if d == 2 else "norm"
                dve.wait_ge(n[done], NCH)

            def stage(l, par, col):
                return V.tensor_copy(gidx[par][:, :], GATHER[l][:, bass.ds(col, U)])

            def messages(l, c, par, col):
                e = ed[l]
                if l == 0:
                    own.did(V.tensor_tensor(v3(basis[:, :]), v3(rows[par][:, 0:U * D]),
                                            spread(ew[:, bass.ds(col, U)]), ALU.mult))
                    own.settle()
                    V.tensor_tensor(v3(raw[:, :]), v3(basis[:, :]), w0[:, None, :].to_broadcast([P, U, D]),
                                    ALU.mult).then_inc(e["raw"], 1)
                elif l == 1:
                    uv = attr2[:, bass.ds(col * 2, 2 * U)]
                    hats = small[:, 0:8 * U]
                    for k in range(4):
                        own.did(V.tensor_scalar(v3(hats, 4)[:, :, k], uv, -1.0 + 2.0 * k / 3.0, 1.5,
                                                ALU.subtract, ALU.mult))
                    own.settle()
                    own.did(V.scalar_tensor_tensor(hats, hats, -1.0, hats, ALU.mult, ALU.min))
                    own.settle()
                    own.did(V.tensor_scalar(hats, hats, 1.0, 0.0, ALU.add, ALU.max))
                    own.settle()
                    hv = hats.rearrange("p (u c n) -> p u c n", c=2, n=4)
                    own.did(V.tensor_tensor(basis[:, :].rearrange("p (u a b) -> p u a b", a=4, b=4),
                                            hv[:, :, 0, :, None].to_broadcast([P, U, 4, 4]),
                                            hv[:, :, 1, None, :].to_broadcast([P, U, 4, 4]), ALU.mult))
                    own.settle()
                    for m in range(7):
                        dve.wait_ge(e["prod"], 14 * c + (7 * par + m + 1))
                        V.tensor_tensor(v3(prod[:, m * 512:(m + 1) * 512]), v3(psP[m % 2][:, :]),
                                        spread(basis[:, 32 * m:32 * m + 32]), ALU.mult).then_inc(e["used"], 1)
                    dve.wait_ge(e["used"], 14 * c + (7 * par + 7))
                    V.tensor_reduce(v3(raw[:, :]), prod[:, :].rearrange("p (u k o) -> p u o k", k=D, o=D),
                                    AX.X, ALU.add).then_inc(e["raw"], 1)
                elif l == 2:
                    dve.wait_ge(rev_in[par], 16 * c + 16)
                    for m in range(8):
                        s, q = m // 4, m % 4
                        tiles = min(4, U - 4 * q)
                        dve.wait_ge(e["prod"], 16 * c + (8 * par + m + 1))
                        o = s * CW + q * 288
                        ps = psP[m % 2][:, 0:tiles * 72].rearrange("p (u t o) -> p u t o", t=A9, o=HALF)
                        pr = prod[:, o:o + tiles * 72].rearrange("p (u t o) -> p u t o", t=A9, o=HALF)
                        at = (rev8[par][:, 4 * q * T2:(4 * q + tiles) * T2] if s
                              else attr8[:, bass.ds(col * T2 + 4 * q * T2, T2 * tiles)])
                        V.tensor_tensor(pr[:, :, 0:T2, :], ps[:, :, 0:T2, :],
                                        v3(at, T2)[:, :, :, None].to_broadcast([P, tiles, T2, HALF]), ALU.mult)
                        V.tensor_copy(pr[:, :, T2, :], ps[:, :, T2, :]).then_inc(e["used"], 1)
                    dve.wait_ge(e["used"], 16 * c + (8 * par + 8))
                    for s in range(2):
                        k = V.tensor_reduce(v3(raw[:, :])[:, :, s * HALF:(s + 1) * HALF],
                                            prod[:, s * CW:s * CW + U * 72]
                                            .rearrange("p (u t o) -> p u o t", t=A9, o=HALF), AX.X, ALU.add)
                    k.then_inc(e["raw"], 1)
                else:
                    for m in range(4):
                        tiles = min(4, U - 4 * m)
                        dve.wait_ge(e["prod"], 8 * c + (4 * par + m + 1))
                        av = v3(attr8[:, bass.ds(col * T2 + 4 * m * T2, T2 * tiles)], T2)[:, :, :, None]
                        V.tensor_tensor(prod[:, m * 512:m * 512 + tiles * P]
                                        .rearrange("p (u j h) -> p u j h", j=T2, h=D),
                                        psP[m % 2][:, 0:tiles * P].rearrange("p (u j h) -> p u j h", j=T2, h=D),
                                        av.to_broadcast([P, tiles, T2, D]), ALU.mult).then_inc(e["used"], 1)
                    dve.wait_ge(e["used"], 8 * c + (4 * par + 4))
                    V.tensor_reduce(v3(basis[:, :]), prod[:, 0:CW].rearrange("p (u j h) -> p u h j", j=T2, h=D),
                                    AX.X, ALU.add).then_inc(e["preact"], 1)
            def edge_phase(l):
                e = ed[l]
                for par in range(2):
                    stage(l, par, par * U).then_inc(e["staged"], 1)

                def equal(g):
                    V.tensor_copy(key[:, :], KEY[l][:, bass.ds(g * U, U)]).then_inc(e["key"], 1)
                    dve.wait_ge(e["keyT"], g + 1)
                    V.tensor_tensor(v3(same[:, :], P), v3(psK[:, 0:CW], P), spread(key[:, :], P), ALU.is_equal)\
                        .then_inc(e["same"], 1)

                equal(0)
                with dve.Fori(0, PAIRS) as c:
                    own.begin(c, STEPS[l])
                    for par in range(2):
                        col = (2 * c + par) * U
                        dve.wait_ge(gath[l][par], c * GATH + GATH)
                        stage(l, par, col + AHEAD * U)
                        if l == 2:
                            fv = [v3(feat[:, s * 2 * P:s * 2 * P + U * D]) for s in range(2)]
                            for s in range(2):
                                own.did(V.tensor_tensor(fv[s], v3(rows[par][:, 0:U * D]),
                                                        gains[s][:, None, :].to_broadcast([P, U, D]), ALU.mult))
                            own.settle()
                            for s in range(2):
                                own.did(V.tensor_tensor(fv[s], fv[s], shifts[s][:, None, :].to_broadcast([P, U, D]),
                                                        ALU.add))
                            own.settle()
                            V.tensor_scalar(feat[:, :], feat[:, :], 0.0, None, ALU.max).then_inc(e["feat"], 1)
                        messages(l, c, par, col)
                        if l < 2:
                            dve.wait_ge(e["same"], 2 * c + (par + 1))
                            if l == 1:
                                dve.wait_ge(e["raw"], 2 * c + (par + 1))
                            before, first = small[:, 0:U], small[:, U:2 * U]
                            own.did(V.tensor_tensor(v3(prod[:, 0:CW], P), v3(same[:, :], P),
                                                    lower[:, None, :].to_broadcast([P, U, P]), ALU.mult))
                            own.did(V.tensor_scalar(first, key[:, :], pad_row[:, :], None, ALU.subtract))
                            own.settle()
                            own.did(V.tensor_reduce(before, v3(prod[:, 0:CW], P), AX.X, ALU.add))
                            own.settle()
                            own.did(V.scalar_tensor_tensor(first, before, 0.0, first, ALU.is_equal, ALU.mult))
                            own.settle()
                            own.did(V.tensor_scalar(sidx[par][:, :], first, pad_row[:, :], None, ALU.add))
                            own.settle()
                            own.did(V.tensor_copy(TO[l][:, bass.ds(col, U)], sidx[par][:, :]))
                        else:
                            own.did(V.tensor_copy(sidx[par][:, :], TO[l][:, bass.ds(col, U)]))
                        dve.wait_ge(e["sum"], 2 * c + (par + 1))
                        V.tensor_copy(msgs[par][:, :], psM[:, 0:U * D]).then_inc(e["msg"], 1)
                        if l == 2 and par:
                            root(c)
                        equal(2 * c + (par + 1))
                        for s in range(2):
                            dve.wait_ge(scat[l][s], c * (2 * SCAT) + (FREE + par * SCAT))
                own.end(PAIRS)

            def root(c):
                w = RB * P
                hs, xs = h[:, bass.ds(c * w, w)], x[:, bass.ds(c * w, w)]
                for s in range(2):
                    r = rt[:, s * w:(s + 1) * w]
                    own.did(V.tensor_tensor(v3(r), v3(hs), gains[s][:, None, :].to_broadcast([P, RB * 8, D]), ALU.mult))
                    own.settle()
                    own.did(V.tensor_tensor(v3(r), v3(r), shifts[s][:, None, :].to_broadcast([P, RB * 8, D]), ALU.add))
                    own.settle()
                    V.tensor_scalar(r, r, 0.0, None, ALU.max).then_inc(rt_s["feat"], 1)
                own.did(V.tensor_tensor(v3(xs), v3(xs), bias16[:, None, :].to_broadcast([P, RB * 8, D]), ALU.add))
                own.settle()
                dve.wait_ge(rt_s["root"], c + 1)
                own.did(V.tensor_tensor(xs, xs, psK[:, 0:w], ALU.add))
                own.settle()

            for l in range(4):
                node_phase(l)
                edge_phase(l)
                if l == 1:
                    dve.wait_ge(w4_psum, 1)
                    for v in range(8):
                        k = V.tensor_scalar(W4[:, v * 256:(v + 1) * 256], psM[:, 0:256], rowmask[:, v:v + 1], NORM_LIN,
                                            ALU.mult, ALU.mult)
                    k.then_inc(w4_ready, 1)

            def halved(c, q):
                dve.wait_ge(up["half"], c * QUADS + (q + 1))
                k = V.tensor_reduce(v3(tD[:, 64 * q:64 * q + 64]), products(q)[1].rearrange("p u i k -> p u k i"),
                                    AX.X, ALU.add)
                if q == QUADS - 1:
                    k.then_inc(up["preact"], 1)
                return k

            def finish(c):
                dve.wait_ge(up["resid"], c + 1)
                dve.wait_ge(up["update"], c + 1)
                xs = step_of(x, c)
                V.scalar_tensor_tensor(xs, psK[:, 0:CW], NORM_LIN, xs, ALU.mult, ALU.add).then_inc(up["done"], 1)

            def update(c, first):
                for q in range(QUADS):
                    dve.wait_ge(up["prod"], c * QUADS + (q + 1))
                    V.tensor_tensor(v3(wide[q % 2]), v3(psQ[q % 2]), spread(h[:, bass.ds(c * CW + 64 * q, 64)]),
                                    ALU.mult).then_inc(up["used"], 1)
                    if q == 1 and not first:
                        dve.wait_ge(up["silu"], c)
                    if q:
                        halved(c, q - 1)
                    if q == QUADS - 4 and not first:
                        finish(c - 1)
                halved(c, QUADS - 1)

            update(0, True)
            with dve.Fori(1, NCH) as c:
                update(c, False)
            finish(NCH - 1)


_INS = ["x", "src", "dst", "edge_attr_2", "edge_attr_8", "edge_attr_8_reversed", "edge_weight", "node_vec1", "L0_gnn_weight",
        "L0_gnn_self_loop_weight", "L1_gnn_weight", "L2_gnn_ln_g_n", "L2_gnn_ln_b_n", "L2_gnn_We_n",
        "L2_gnn_be_n", "L2_gnn_Wr_n", "L2_gnn_b_n", "L2_gnn_ln_g_r", "L2_gnn_ln_b_r", "L2_gnn_We_r",
        "L2_gnn_be_r", "L2_gnn_Wr_r", "L2_gnn_b_r", "L3_gnn_W_msg_tp", "L3_gnn_W_msg_lin",
        "L3_gnn_W_upd_tp", "L3_gnn_W_upd_lin"]


def kernel(**inputs):
    import numpy as _np
    import concourse.bacc as _bacc
    from concourse import mybir as _mybir
    from concourse.bass_utils import run_bass_kernel_spmd as _run

    nc = _bacc.Bacc("TRN2", target_bir_lowering=False, num_devices=1)
    inputs["edge_attr_8_reversed"] = _np.ascontiguousarray(_np.asarray(inputs["edge_attr_8"])[::-1])
    arrays, args = {}, []
    for name in _INS:
        a = _np.ascontiguousarray(inputs[name])
        a = a.reshape(a.shape or (1,))
        arrays[f"in_{name}_dram"] = a
        args.append(nc.dram_tensor(f"in_{name}_dram", a.shape, _mybir.dt.from_np(a.dtype), kind="ExternalInput").ap())
    out = nc.dram_tensor("out_0_dram", (N, D), _mybir.dt.float32, kind="ExternalOutput").ap()
    build_gnn(nc, *args, out)
    r = _run(nc, [arrays], core_ids=[0])
    return r.results[0]["out_0_dram"]
```

```python
import concourse.bass as bass
from concourse import mybir
from contextlib import ExitStack


P = 128
N, E, D = 100000, 50000, 16
COLS = 784
NPAD = P * COLS
ROWS = NPAD + P
CH = 112
NCH = COLS // CH
CW = CH * D
RB = 7
BLK = CW // P
FULL = N // COLS
LAST = N - FULL * COLS
WIDE = FULL // 16 * 16
ZW = 448
U = 14
TILES = 392
GROUPS = TILES // U
PAIRS = GROUPS // 2
ET = E // P
REST = E - ET * P
AHEAD = 2
ICOLS = TILES + AHEAD * U
T2 = 8
A9 = T2 + 1
HALF = 8
EPS = 1e-5


class Steps:

    def __init__(self, eng, sem):
        self.eng, self.sem, self.base, self.turn, self.per, self.k = eng, sem, 0, 0, 0, 0

    def begin(self, turn, per):
        self.turn, self.per, self.k = turn, per, 0

    def end(self, turns):
        assert self.k == self.per, (self.k, self.per)
        self.base += self.per * turns
        self.begin(0, 0)

    def did(self, instruction):
        self.k += 1
        instruction.then_inc(self.sem, 1)

    def settle(self):
        self.eng.wait_ge(self.sem, self.turn * self.per + (self.base + self.k))


def build_gnn(nc, x_in, src_in, dst_in, attr2_in, attr8_in, attr8_rev_in, ew_in, w0_in, slw_in, w1_in,
              g_n_in, b_n_in, We_n_in, be_n_in, Wr_n_in, bias_n_in,
              g_r_in, b_r_in, We_r_in, be_r_in, Wr_r_in, bias_r_in,
              Wmsg_in, Wmlin_in, Wupd_in, Wulin_in, out):
    f32, i32 = mybir.dt.float32, mybir.dt.int32
    ALU, ACT, AX = mybir.AluOpType, mybir.ActivationFunctionType, mybir.AxisListType
    NORM_MSG = float((D * T2) ** -0.5)
    NORM_UPD = float((D * D) ** -0.5)
    NORM_LIN = float(D ** -0.5)

    ctx = ExitStack()
    with ctx:
        def sb(name, shape, dt=f32):
            return ctx.enter_context(nc.sbuf_tensor(name, shape, dt))

        def sem(name):
            return ctx.enter_context(nc.semaphore(name))

        table = nc.dram_tensor("table", (ROWS, D), f32)
        accum = [[nc.dram_tensor(f"accum{l}_{s}", (ROWS, D), f32) for s in range(2)]
                 for l in range(4)]

        x = sb("x", [P, COLS * D])
        h = sb("h", [P, COLS * D])
        src = sb("src", [P, ICOLS], i32)
        dst = sb("dst", [P, ICOLS], i32)
        to_src = sb("to_src", [P, TILES], i32)
        to_dst = sb("to_dst", [P, TILES], i32)
        ew = sb("ew", [P, TILES])
        attr2 = sb("attr2", [P, TILES * 2])
        attr8 = sb("attr8", [P, TILES * T2])
        rev8 = [sb(f"rev8_{p}", [P, U * T2]) for p in range(2)]
        gidx = [sb(f"gidx{p}", [P, U], i32) for p in range(2)]
        sidx = [sb(f"sidx{p}", [P, U], i32) for p in range(2)]
        rows = [sb(f"rows{p}", [P, 2 * P]) for p in range(2)]
        msgs = [sb(f"msgs{p}", [P, U * D]) for p in range(2)]
        key = sb("key", [P, U])
        same = sb("same", [P, CW])
        tB = sb("tB", [P, CW])
        prod = sb("prod", [P, 2 * CW])
        raw = sb("raw", [P, U * D])
        small = sb("small", [P, 8 * CH])
        basis = sb("basis", [P, U * D])
        featT = sb("featT", [P, 4 * P])
        ident = sb("ident", [P, P])
        lower = sb("lower", [P, P])
        rowmask = sb("rowmask", [P, 8])
        pad_row = sb("pad_row", [P, 1])
        eps = sb("eps", [P, 1])
        w0 = sb("w0", [P, D])
        slw1 = sb("slw1", [P, 1])
        gains = [sb(f"gain{s}", [P, 1]) for s in range(2)]
        shifts = [sb(f"shift{s}", [P, 1]) for s in range(2)]
        bias16 = sb("bias16", [P, D])
        W1 = sb("W1", [P, 4 * 512])
        W2 = [sb(f"W2_{s}", [P, 2 * 288]) for s in range(2)]
        W3 = sb("W3", [P, 2 * 512])
        Wroot = [sb(f"Wroot{s}", [P, P]) for s in range(2)]
        W4 = W1
        Wfin = sb("Wfin", [P, P])
        mlinT = sb("mlinT", [D, P])
        upd = sb("upd", [D, D * D])

        zeros = sb("zeros", [P, ZW])
        extra = sb("extra", [P, 512])
        rt = sb("rt", [P, 2 * CW])

        psK = ctx.enter_context(nc.psum_tensor("psK", [P, 2048], f32))
        psX = ctx.enter_context(nc.psum_tensor("psX", [P, 2048], f32))
        psT = psX[:, 0:512]
        psP = [psX[:, 512:1024], psX[:, 1024:1536]]
        psM = psX[:, 1536:2048]
        psQ = [psX[:, 0:1024], psX[:, 1024:2048]]

        x_first = sem("x_first")
        x_loaded = sem("x_loaded")
        loaded = sem("loaded")
        weights = sem("weights")
        cleared = sem("cleared")
        masks = sem("masks")
        w4_psum = sem("w4_psum")
        w4_ready = sem("w4_ready")
        zeroed = [sem(f"zeroed{l}") for l in range(4)]
        stored = sem("stored")
        names = ("staged",
                 "key",
                 "keyT",
                 "same",
                 "bandT",
                 "bandS",
                 "prod",
                 "used",
                 "preact",
                 "raw",
                 "sum",
                 "msg")
        lacks = [("bandT", "bandS", "prod", "used", "preact"), ("preact",), ("preact",), ()]
        ed = [{n: sem(f"e{l}_{n}") for n in names if n not in lacks[l]} for l in range(4)]
        pool_go = sem("pool_go")
        rev_in = [sem(f"rev_in{p}") for p in range(2)]
        rev_rest = sem("rev_rest")
        gath = [[sem(f"e{l}_gath{p}") for p in range(2)] for l in range(4)]
        scat = [[sem(f"e{l}_scat{s}") for s in range(2)] for l in range(4)]
        nnames = ("loadA", "loadB",
                  "looped",
                  "takenA", "takenB",
                  "relu",
                  "mean",
                  "center", "center2",
                  "square", "square2",
                  "varsum", "varsum2",
                  "sdev", "sdev2",
                  "inv2",
                  "norm", "norm2",
                  "store")
        lacks = [nnames[0:6], ("mean",), ("looped", "mean", "varsum", "sdev", "norm"),
                 ("relu", "looped", "mean")]
        nd = [{n: sem(f"n{l}_{n}") for n in nnames if (l == 2 or n[-1] != "2") and n not in lacks[l]}
              for l in range(4)]
        unames = ("loadA", "loadB",
                  "total",
                  "totalT", "totalS",
                  "prod", "used",
                  "half",
                  "preact", "silu",
                  "siluT", "siluS",
                  "update", "moved",
                  "resid",
                  "done")
        up = {n: sem(f"u_{n}") for n in unames}
        rnames = ("rows",
                  "bandT",
                  "bandS",
                  "root")
        root_s = {n: sem(f"r_{n}") for n in rnames}
        dve_go = sem("dve_go")
        dve_step = sem("dve_step")

        def v3(ap, f=D):
            return ap.rearrange("p (u f) -> p u f", f=f)

        def node_rows(t):
            return t.ap()[0:NPAD, :].rearrange("(p c) f -> p (c f)", p=P)

        mean, var, sdev, inv, mean2, var2, sdev2, inv2 = [small[:, i * CH:(i + 1) * CH] for i in range(8)]
        floor2, total2 = sdev, inv
        tA, tC, tD = same, prod[:, 0:CW], prod[:, CW:2 * CW]
        uA, uB = rt[:, 0:CW], rt[:, CW:2 * CW]
        BUILT = 9
        MASKS = BUILT + 11
        BEHIND = 3
        own_peeled = [(1, 1), (2, 1), None, (1, 1)]
        own_turn = [2, 3, None, 2]
        STEPS = [14, 26, 4, 2]
        LOADS = 16 * 12
        WEIGHTS = 16 * (2 + 8 * 14 + 1)
        CLEARED = 9

        QUADS = CH // 4
        DEEP = 4
        LAG = DEEP - 1
        wide = [attr8[:, i * 1024:(i + 1) * 1024] for i in range(3)] + [W3[:, :]]
        halves = [t[:, 0:512] for t in (W2[0], W2[1], attr2, extra)]

        def products(q):
            return (wide[q % DEEP].rearrange("p (u i k) -> p u i k", i=D, k=D),
                    halves[q % DEEP].rearrange("p (u i k) -> p u i k", i=D // 2, k=D))

        block = ctx.enter_context(nc.Block())

        GATHER = [src, dst, src, dst]
        KEY = [dst, src, dst, src]
        TO = [to_dst, to_src, to_dst, to_src]
        GATH = 16 * U
        SCAT = 16 * U // 2
        FREE = 16

        @block.sync
        def _(sp):
            def load(o, i, signal=loaded):
                sp.dma_start(o, i).then_inc(signal, 16)

            def weight(o, i):
                load(o, i, weights)

            def zero(l, start, cols, which=(0, 1)):
                for s in which:
                    sp.dma_start(node_rows(accum[l][s])[:, bass.ds(start * D, cols * D)]
                                 .rearrange("p (k w) -> p k w", w=ZW),
                                 zeros[:, None, :].to_broadcast([P, cols * D // ZW, ZW]))\
                        .then_inc(zeroed[l], 16)

            for signal, cols in ((x_first, slice(0, CW)), (x_loaded, slice(CW, COLS * D))):
                for a, b in ((0, WIDE), (WIDE, FULL)):
                    sp.dma_start(x[a:b, cols], x_in[a * COLS:b * COLS, :]
                                 .rearrange("(p c) f -> p (c f)", c=COLS)[:, cols]).then_inc(signal, 16)
                end = min(cols.stop, LAST * D)
                sp.dma_start(x[FULL:FULL + 1, cols.start:end],
                             x_in[FULL * COLS:N, :].rearrange("(p c) f -> p (c f)", p=1)[:, cols.start:end])\
                    .then_inc(signal, 16)
            sp.wait_ge(cleared, 1)
            sp.dma_start(x[FULL:FULL + 1, LAST * D:].rearrange("p (k w) -> p k w", k=D),
                         zeros[FULL:FULL + 1, None, 0:COLS - LAST].to_broadcast([1, D, COLS - LAST]))\
                .then_inc(x_loaded, 16)
            sp.dma_start(table.ap()[NPAD:ROWS, :], zeros[:, 0:D]).then_inc(nd[0]["store"], 16)
            sp.wait_ge(cleared, CLEARED)
            sp.wait_ge(masks, MASKS)
            with nc.allow_non_contiguous_dma(reason="the last column of edges and small weights"):
                for t, a in ((src, src_in), (dst, dst_in), (ew, ew_in)):
                    load(t[:, 0:ET], a[0:ET * P].rearrange("(p c) -> p c", p=P))
                    load(t[0:REST, ET:ET + 1], a[ET * P:E].rearrange("(p c) -> p c", c=1))
                a2, a8 = v3(attr2[:, :], 2), v3(attr8[:, :], T2)
                load(a2[:, 0:ET, :], attr2_in[0:ET * P, :].rearrange("(p c) f -> p c f", p=P))
                load(a2[0:REST, ET, :], attr2_in[ET * P:E, :])
                load(a8[:, 0:ET, :], attr8_in[0:ET * P, :].rearrange("(p c) f -> p c f", p=P))
                load(a8[0:REST, ET, :], attr8_in[ET * P:E, :])
                load(w0[:, :], w0_in[None, :].to_broadcast([P, D]))
                load(slw1[:, :], slw_in[None, :].to_broadcast([P, 1]))
            zero(0, 0, COLS, (0,))
            with nc.allow_non_contiguous_dma(reason="small weights"):
                weight(bias16[:, 0:HALF], bias_n_in[None, :].to_broadcast([P, HALF]))
                weight(bias16[:, HALF:D], bias_r_in[None, :].to_broadcast([P, HALF]))
                w1v = w1_in.rearrange("a b i o -> i (a b) o")
                w3v = Wmsg_in.rearrange("i j h -> i (j h)")
                for v in range(8):
                    band = slice(D * v, D * v + D)
                    c1 = (v // 2) * 512 + (v % 2) * 256
                    weight(v3(W1[:, :])[band, c1 // D:c1 // D + D, :], w1v)
                    c3 = v * P
                    weight(W3[band, c3:c3 + P], w3v)
                    for s, (We, be, Wr) in enumerate(((We_n_in, be_n_in, Wr_n_in),
                                                      (We_r_in, be_r_in, Wr_r_in))):
                        c2 = v * A9
                        w2 = v3(W2[s][:, :], HALF)
                        weight(w2[band, c2:c2 + T2, :], We.rearrange("t (i o) -> i t o", o=HALF))
                        weight(w2[band, c2 + T2, :], be.rearrange("(i o) -> i o", o=HALF))
                        weight(Wroot[s][band, v * D + s * HALF:v * D + (s + 1) * HALF], Wr)
                    for t, values in zip(gains + shifts, (g_n_in, g_r_in, b_n_in, b_r_in)):
                        weight(t[band, :], values.rearrange("(f o) -> f o", o=1))
                    weight(Wfin[band, v * D:v * D + D], Wulin_in)
                    weight(mlinT[:, band], Wmlin_in.rearrange("q h -> h q"))
                weight(v3(upd[:, :]), Wupd_in.rearrange("i h k -> h i k"))
            sp.wait_ge(nd[0]["store"], 16 * (NCH + 1))
            zero(0, 0, COLS, (1,))

            for l in range(4):
                if l == 2:
                    rev = attr8_rev_in[0:ET * P, :].rearrange("(p c) f -> p (c f)", p=P)

                    def reverse(par, col, cols=U):
                        sp.dma_start(rev8[par][:, 0:cols * T2], rev[:, bass.ds(col * T2, cols * T2)])\
                            .then_inc(rev_in[par], 16)

                    reverse(0, 0)
                    reverse(1, U)
                piece = COLS // PAIRS
                if l in (0, 1):
                    with sp.Fori(0, PAIRS) as c:
                        sp.wait_ge(ed[l]["msg"], 2 * c + 1)
                        zero(l + 1, c * piece, piece)
                if l == 2:
                    zero(3, 0, piece)
                    with sp.Fori(1, PAIRS - 1) as c:
                        for par in range(2):
                            sp.wait_ge(ed[l]["msg"], 2 * c + (par - 1))
                            reverse(par, (2 * c + par) * U)
                        zero(3, c * piece, piece)
                    sp.wait_ge(ed[l]["msg"], GROUPS - 3)
                    reverse(0, (GROUPS - 2) * U)
                    sp.wait_ge(ed[l]["msg"], GROUPS - 2)
                    left = ET - (GROUPS - 1) * U
                    sp.dma_start(rev8[1][0:REST, left * T2:(left + 1) * T2], attr8_rev_in[ET * P:E, :])\
                        .then_inc(rev_rest, 16)
                    sp.wait_ge(rev_rest, 16)
                    reverse(1, (GROUPS - 1) * U, left)
                    zero(3, (PAIRS - 1) * piece, piece)
                sp.wait_ge(ed[l]["same"], GROUPS + 1)
                n = nd[l + 1] if l < 3 else up
                freed = (n["takenA"], n["takenB"]) if l < 3 else (n["totalT"], n["total"])
                arrived = (n["loadA"], n["loadB"])

                def fetch(s, c):
                    sp.dma_start((tA, tB)[s][:, :], node_rows(accum[l][s])[:, bass.ds(c * CW, CW)])\
                        .then_inc(arrived[s], 16)

                for s in range(2):
                    sp.wait_ge(scat[l][s], FREE + SCAT * GROUPS)
                    fetch(s, 0)
                with sp.Fori(1, NCH) as c:
                    for s in range(2):
                        sp.wait_ge(freed[s], c)
                        fetch(s, c)

        @block.gpsimd
        def _(pool):
            pool.memset(ident[:, :], 0.0).then_inc(masks, 1)
            pool.memset(lower[:, :], 1.0).then_inc(masks, 1)
            pool.memset(rowmask[:, :], 1.0).then_inc(masks, 1)
            for t in (src, dst):
                pool.iota(t[:, ET:ICOLS], pattern=[[0, ICOLS - ET]], base=NPAD, channel_multiplier=1)\
                    .then_inc(masks, 1)
            pool.wait_ge(masks, 3)
            pool.affine_select(out=ident[:, :], in_=ident[:, :], compare_op=ALU.not_equal, fill=1.0, base=0,
                               pattern=[[-1, P]], channel_multiplier=1).then_inc(masks, 1)
            pool.affine_select(out=lower[:, :], in_=lower[:, :], compare_op=ALU.is_gt, fill=0.0, base=0,
                               pattern=[[-1, P]], channel_multiplier=1).then_inc(masks, 1)
            pool.affine_select(out=rowmask[:, :], in_=rowmask[:, :], compare_op=ALU.is_ge, fill=0.0, base=0,
                               pattern=[[-D, 8]], channel_multiplier=1).then_inc(masks, 1)
            pool.wait_ge(masks, BUILT - 1)
            pool.affine_select(out=rowmask[:, :], in_=rowmask[:, :], compare_op=ALU.is_ge, fill=0.0, base=D - 1,
                               pattern=[[D, 8]], channel_multiplier=-1).then_inc(masks, 1)
            for t in (W1, W2[0], W2[1], W3, Wroot[0], Wroot[1], Wfin, rows[0], rows[1], rev8[0], rev8[1]):
                pool.memset(t[:, :], 0.0).then_inc(masks, 1)

            for l in range(4):
                e = ed[l]

                def gather(par, u):
                    pool.indirect_dma_start(
                        out=rows[par][:, u * D:(u + 1) * D], out_offset=None, in_=table.ap(),
                        in_offset=bass.IndirectOffsetOnAxis(ap=gidx[par][:, u:u + 1], axis=0))\
                        .then_inc(gath[l][par], 16)

                def scatter(par, turn, and_gather):
                    for u in range(U):
                        pool.wait_ge(scat[l][u % 2], turn * (2 * SCAT) + (FREE + par * SCAT + 16 * (u // 2)))
                        pool.sem_inc(pool_go, 1)
                        pool.indirect_dma_start(
                            out=accum[l][u % 2].ap(),
                            out_offset=bass.IndirectOffsetOnAxis(ap=sidx[par][:, u:u + 1], axis=0),
                            in_=msgs[par][:, u * D:(u + 1) * D], in_offset=None, compute_op=ALU.add)\
                            .then_inc(scat[l][u % 2], 16)
                        if and_gather:
                            gather(par, u)

                pool.wait_ge(cleared, CLEARED)
                for s in range(2):
                    pool.dma_start(accum[l][s].ap()[NPAD:ROWS, :], zeros[:, 0:D]).then_inc(scat[l][s], FREE)
                n = nd[l]

                def scale2(c):
                    hs = h[:, bass.ds(c * CW, CW)]
                    pool.wait_ge(n["inv2"], c + 1)
                    pool.sem_inc(pool_go, 1)
                    nc.gpsimd.tensor_tensor(v3(hs), v3(hs), inv2[:, :, None].to_broadcast([P, CH, D]), ALU.mult)\
                        .then_inc(n["norm2"], 1)

                if l == 0:
                    with pool.Fori(0, NCH) as c:
                        pool.wait_ge(n["mean"], c + 1)
                        pool.sem_inc(pool_go, 1)
                        nc.gpsimd.tensor_tensor(v3(h[:, bass.ds(c * CW, CW)]), v3(x[:, bass.ds(c * CW, CW)]),
                                                mean[:, :, None].to_broadcast([P, CH, D]), ALU.subtract)\
                            .then_inc(n["center"], 1)
                else:
                    def add(c):
                        xs = x[:, bass.ds(c * CW, CW)]
                        to, sums = (uA, uB) if l == 1 else (xs, xs)
                        pool.wait_ge(n["loadA"], 16 * c + 16)
                        pool.sem_inc(pool_go, 1)
                        if l == 1:
                            pool.wait_ge(n["looped"], c + 1)
                            pool.sem_inc(pool_go, 1)
                        nc.gpsimd.tensor_tensor(to, to, tA[:, :], ALU.add).then_inc(n["takenA"], 1)
                        pool.wait_ge(n["loadB"], 16 * c + 16)
                        pool.sem_inc(pool_go, 1)
                        pool.wait_ge(n["takenA"], c + 1)
                        pool.sem_inc(pool_go, 1)
                        if l == 1:
                            pool.wait_ge(n["relu"], c)
                            pool.sem_inc(pool_go, 1)
                        nc.gpsimd.tensor_tensor(sums, to, tB[:, :], ALU.add).then_inc(n["takenB"], 1)
                    if l == 2:
                        with pool.Fori(1, BEHIND) as c:
                            add(c)
                        with pool.Fori(BEHIND, NCH) as c:
                            add(c)
                            scale2(c - BEHIND)
                        for c in range(NCH - BEHIND, NCH):
                            scale2(c)
                    else:
                        with pool.Fori(1, NCH) as c:
                            add(c)
                pool.wait_ge(nd[l]["store"], 16 * (NCH + (l == 0)))
                pool.wait_ge(e["staged"], 2)
                pool.sem_inc(pool_go, 1)
                for par in range(2):
                    for u in range(U):
                        gather(par, u)
                pool.wait_ge(zeroed[l], 16 * 2 * (PAIRS if l else 1))
                with pool.Fori(0, PAIRS - 1) as c:
                    for par in range(2):
                        pool.wait_ge(e["msg"], 2 * c + (par + 1))
                        pool.sem_inc(pool_go, 1)
                        scatter(par, c, True)
                for par in range(2):
                    pool.wait_ge(e["msg"], 2 * (PAIRS - 1) + par + 1)
                    scatter(par, PAIRS - 1, False)

            def total():
                nc.gpsimd.tensor_tensor(tA[:, :], tA[:, :], tB[:, :], ALU.add).then_inc(up["total"], 1)

            def finish(c):
                xs = x[:, bass.ds(c * CW, CW)]
                pool.wait_ge(up["moved"], c + 1)
                pool.sem_inc(pool_go, 1)
                pool.wait_ge(up["resid"], c + 1)
                pool.sem_inc(pool_go, 1)
                nc.gpsimd.tensor_tensor(xs, xs, tC, ALU.add).then_inc(up["done"], 1)

            def update(c, first, last):
                xs = x[:, bass.ds(c * CW, CW)]
                for q in range(QUADS):
                    if q == 8 and not last:
                        pool.wait_ge(up["loadA"], 16 * c + 32)
                        pool.sem_inc(pool_go, 1)
                        pool.wait_ge(up["loadB"], 16 * c + 32)
                        total()
                    if q == 14 and not first:
                        finish(c - 1)
                    if q == 21:
                        nc.gpsimd.tensor_tensor(xs, xs, h[:, bass.ds(c * CW, CW)], ALU.add).then_inc(up["resid"], 1)
                    w, hf = products(q)
                    pool.wait_ge(up["used"], c * QUADS + (q + 1))
                    nc.gpsimd.tensor_tensor(hf, w[:, :, 0:8, :], w[:, :, 8:16, :], ALU.add).then_inc(up["half"], 1)

            update(0, True, False)
            with pool.Fori(1, NCH - 1) as c:
                update(c, False, False)
            update(NCH - 1, False, True)

        @block.tensor
        def _(pe):
            pe.wait_ge(masks, MASKS)

            def root_rows(c):
                pe.wait_ge(ed[2]["same"], 2 * c + 2)
                pe.wait_ge(root_s["rows"], c + 1)
                for b in range(RB):
                    k = nc.tensor.transpose(psK[:, b * P:(b + 1) * P],
                                            rt[:, (2 * RB + b) * P:(2 * RB + b + 1) * P], ident[:, :])
                k.then_inc(root_s["bandT"], 1)

            def root_products(c):
                pe.wait_ge(root_s["bandS"], c + 1)
                for b in range(RB):
                    for s in range(2):
                        k = nc.tensor.matmul(psK[:, b * P:(b + 1) * P],
                                             rt[:, (s * RB + b) * P:(s * RB + b + 1) * P],
                                             Wroot[s][:, :], start=s == 0, stop=s == 1)
                k.then_inc(root_s["root"], 1)

            for l in range(4):
                e = ed[l]

                def key_rows(g):
                    pe.wait_ge(e["key"], g + 1)
                    for u in range(U):
                        k = nc.tensor.transpose(psK[:, u * P:(u + 1) * P],
                                                key[:, u:u + 1].to_broadcast([P, P]), ident[:, :])
                    k.then_inc(e["keyT"], 1)

                if l == 1:
                    pe.wait_ge(weights, WEIGHTS)
                key_rows(0)
                with pe.Fori(0, PAIRS) as c:
                    for par in range(2):
                        if l:
                            pe.wait_ge(gath[l][par], c * GATH + GATH)
                            for b in range(2):
                                k = nc.tensor.transpose(psT[:, b * P:(b + 1) * P],
                                                        rows[par][:, b * P:(b + 1) * P], ident[:, :])
                            k.then_inc(e["bandT"], 1)
                            if l == 2 and par:
                                root_rows(c)
                            pe.wait_ge(e["bandS"], 2 * c + (par + 1))
                            if l == 1:
                                parts = [(m // 4, W1[:, (m % 4) * 512:(m % 4 + 1) * 512]) for m in range(7)]
                            elif l == 3:
                                parts = [(m // 2, W3[:, (m % 2) * 512:(m % 2 + 1) * 512]) for m in range(4)]
                            else:
                                parts = [(2 * s + m // 2, W2[s][:, (m % 2) * 288:(m % 2 + 1) * 288])
                                         for s in range(2) for m in range(4)]
                            n = len(parts)
                            for m, (b, w) in enumerate(parts):
                                if m >= 2:
                                    pe.wait_ge(e["used"], c * (2 * n) + (par * n + m - 1))
                                nc.tensor.matmul(psP[m % 2][:, 0:w.shape[1]], featT[:, b * P:(b + 1) * P], w,
                                                 start=True, stop=True).then_inc(e["prod"], 1)
                            if l == 2 and par:
                                root_products(c)
                        pe.wait_ge(e["same"], 2 * c + (par + 1))
                        pe.wait_ge(e["raw"], 2 * c + (par + 1))
                        for u in range(U):
                            k = nc.tensor.matmul(psM[:, u * D:(u + 1) * D], same[:, u * P:(u + 1) * P],
                                                 raw[:, u * D:(u + 1) * D], start=True, stop=True)
                        k.then_inc(e["sum"], 1)
                        key_rows(2 * c + (par + 1))
                if l == 1:
                    pe.wait_ge(e["msg"], GROUPS)
                    nc.tensor.matmul(psM[:, 0:256], mlinT[:, :], upd[:, :], start=True, stop=True)\
                        .then_inc(w4_psum, 1)
                    pe.wait_ge(w4_ready, 1)

            def sum_rows(c):
                pe.wait_ge(up["total"], c + 1)
                for b in range(BLK):
                    k = nc.tensor.transpose(psK[:, b * P:(b + 1) * P], tA[:, b * P:(b + 1) * P], ident[:, :])
                k.then_inc(up["totalT"], 1)

            def silu_rows(c):
                pe.wait_ge(up["silu"], 2 * c + 2)
                for b in range(BLK):
                    k = nc.tensor.transpose(psK[:, b * P:(b + 1) * P], tC[:, b * P:(b + 1) * P], ident[:, :])
                k.then_inc(up["siluT"], 1)

            def step_update(c):
                pe.wait_ge(up["siluS"], c + 1)
                for b in range(BLK):
                    k = nc.tensor.matmul(psK[:, b * P:(b + 1) * P], rt[:, CW + b * P:CW + (b + 1) * P], Wfin[:, :],
                                         start=True, stop=True)
                k.then_inc(up["update"], 1)

            def step(c, first, last):
                for q in range(QUADS):
                    if q % (QUADS // 2) == 0:
                        pe.wait_ge(up["totalS"], 2 * c + (1 + 2 * q // QUADS))
                    if q == 5 and not first:
                        pe.wait_ge(up["totalS"], 2 * c + 2)
                        silu_rows(c - 1)
                    if q == 9 and not first:
                        step_update(c - 1)
                    if q == 15 and not last:
                        if not first:
                            pe.wait_ge(up["moved"], c)
                        else:
                            pe.wait_ge(up["totalS"], 2)
                        sum_rows(c + 1)
                    if not first or q >= 2:
                        pe.wait_ge(up["used"], c * QUADS + (q - 1))
                    for j in range(2):
                        b, m = q // 2, 2 * (q % 2) + j
                        k = nc.tensor.matmul(psQ[q % 2][:, j * 512:(j + 1) * 512], rt[:, b * P:(b + 1) * P],
                                             W4[:, m * 512:(m + 1) * 512], start=True, stop=True)
                    k.then_inc(up["prod"], 1)

            sum_rows(0)
            step(0, True, False)
            with pe.Fori(1, NCH - 1) as c:
                step(c, False, False)
            step(NCH - 1, False, True)
            silu_rows(NCH - 1)
            step_update(NCH - 1)

        @block.scalar
        def _(act):
            def square(n, c, which=""):
                act.wait_ge(n["center" + which], c + 1)
                nc.scalar.activation(tC if which else tD, h[:, bass.ds(c * CW, CW)], ACT.Square)\
                    .then_inc(n["square" + which], 1)

            def root(n, c):
                act.wait_ge(n["varsum"], c + 1)
                nc.scalar.activation(sdev, var, ACT.Sqrt, bias=eps[:, :], scale=1.0 / D).then_inc(n["sdev"], 1)

            def root2(n, c):
                act.wait_ge(n["varsum2"], c + 1)
                nc.scalar.activation(sdev2, total2, ACT.Sqrt).then_inc(n["sdev2"], 1)

            def relu2(n, c):
                nc.scalar.activation(uA, h[:, bass.ds(c * CW, CW)], ACT.Relu).then_inc(n["relu"], 1)

            def self_loop(n, c):
                act.wait_ge(n["takenB"], c)
                nc.scalar.activation(uA, h[:, bass.ds(c * CW, CW)], ACT.Copy, scale=slw1[:, :])\
                    .then_inc(n["looped"], 1)

            def relu(n, c):
                act.wait_ge(n["takenB"], c + 1)
                nc.scalar.activation(tC, uB, ACT.Relu).then_inc(n["relu"], 1)

            def store(n, c, which=""):
                act.wait_ge(n["norm" + which], c + 1)
                act.dma_start(node_rows(table)[:, bass.ds(c * CW, CW)], h[:, bass.ds(c * CW, CW)])\
                    .then_inc(n["store"], 16)

            for d in range(4):
                n, e = nd[d], ed[d]
                if d == 2:
                    def turn2(c):
                        square(n, c)
                        square(n, c - 1, "2")
                        relu2(n, c)

                    square(n, 0)
                    relu2(n, 0)
                    turn2(1)
                    root2(n, 0)
                    turn2(2)
                    with act.Fori(BEHIND, NCH) as c:
                        root2(n, c - 2)
                        turn2(c)
                        store(n, c - BEHIND, "2")
                    root2(n, NCH - 2)
                    square(n, NCH - 1, "2")
                    root2(n, NCH - 1)
                    for c in range(NCH - BEHIND, NCH):
                        store(n, c, "2")
                else:
                    def turn(c, left=2):
                        root(n, c - 1)
                        if d == 1:
                            if left == 2:
                                self_loop(n, c + 2)
                            if left:
                                relu(n, c + 1)
                        square(n, c)
                        store(n, c - 1)

                    if d == 1:
                        act.wait_ge(ed[0]["staged"], 1)
                        nc.scalar.activation(uA, h[:, 0:CW], ACT.Copy, scale=slw1[:, :]).then_inc(n["looped"], 1)
                        self_loop(n, 1)
                        relu(n, 0)
                    square(n, 0)
                    if d == 1:
                        self_loop(n, 2)
                        relu(n, 1)
                    with act.Fori(1, NCH - 2) as c:
                        turn(c)
                    turn(NCH - 2, 1)
                    turn(NCH - 1, 0)
                    root(n, NCH - 1)
                    store(n, NCH - 1)
                if d == 2:
                    act.wait_ge(weights, WEIGHTS)
                if d:
                    with act.Fori(0, PAIRS) as c:
                        for par in range(2):
                            act.wait_ge(e["bandT"], 2 * c + (par + 1))
                            if d == 2:
                                for s in range(2):
                                    k = nc.scalar.activation(featT[:, s * 2 * P:(s + 1) * 2 * P], psT[:, 0:2 * P],
                                                             ACT.Relu, scale=gains[s][:, :], bias=shifts[s][:, :])
                            else:
                                k = nc.scalar.activation(featT[:, 0:2 * P], psT[:, 0:2 * P], ACT.Copy)
                            k.then_inc(e["bandS"], 1)
                            if d == 3:
                                act.wait_ge(e["preact"], 2 * c + (par + 1))
                                nc.scalar.activation(raw[:, :], basis[:, :], ACT.Silu, scale=NORM_MSG)\
                                    .then_inc(e["raw"], 1)
                            if d == 2 and par == 0:
                                nc.scalar.activation(rt[:, 2 * RB * P:3 * RB * P], h[:, bass.ds(c * RB * P, RB * P)],
                                                     ACT.Copy).then_inc(root_s["rows"], 1)
                        if d == 2:
                            act.wait_ge(root_s["bandT"], c + 1)
                            for s in range(2):
                                k = nc.scalar.activation(rt[:, s * RB * P:(s + 1) * RB * P], psK[:, 0:RB * P],
                                                         ACT.Relu, scale=gains[s][:, :], bias=shifts[s][:, :])
                            k.then_inc(root_s["bandS"], 1)

            HW = CW // 2

            def copy_sums(c, half):
                nc.scalar.activation(rt[:, half * HW:(half + 1) * HW], psK[:, half * HW:(half + 1) * HW], ACT.Copy)\
                    .then_inc(up["totalS"], 1)

            def silu(c, half):
                act.wait_ge(up["preact"], 2 * c + (half + 1))
                nc.scalar.activation(tC[:, half * HW:(half + 1) * HW], tD[:, half * HW:(half + 1) * HW], ACT.Silu,
                                     scale=NORM_UPD).then_inc(up["silu"], 1)

            def move(c, last=False):
                act.wait_ge(up["siluT"], c + 1)
                nc.scalar.activation(rt[:, CW:2 * CW], psK[:, 0:CW], ACT.Copy).then_inc(up["siluS"], 1)
                if last:
                    return
                act.wait_ge(up["update"], c + 1)
                nc.scalar.activation(tC, psK[:, 0:CW], ACT.Copy, scale=NORM_LIN).then_inc(up["moved"], 1)

            def store_out(c):
                for a, b in ((0, WIDE), (WIDE, FULL)):
                    act.dma_start(out[a * COLS:b * COLS, :].rearrange("(p c) f -> p (c f)", c=COLS)
                                  [:, bass.ds(c * CW, CW)], x[a:b, bass.ds(c * CW, CW)]).then_inc(stored, 16)

            def step(c, first, last):
                if not first:
                    silu(c - 1, 1)
                    move(c - 1)
                if not last:
                    act.wait_ge(up["totalT"], c + 2)
                    copy_sums(c + 1, 0)
                if not first:
                    act.wait_ge(up["done"], c)
                silu(c, 0)
                if not first:
                    store_out(c - 1)
                if not last:
                    act.wait_ge(up["prod"], c * QUADS + QUADS)
                    copy_sums(c + 1, 1)

            act.wait_ge(up["totalT"], 1)
            copy_sums(0, 0)
            copy_sums(0, 1)
            step(0, True, False)
            with act.Fori(1, NCH - 1) as c:
                step(c, False, False)
            step(NCH - 1, False, True)
            silu(NCH - 1, 1)
            move(NCH - 1, True)
            act.wait_ge(up["done"], NCH)
            store_out(NCH - 1)
            act.dma_start(out[FULL * COLS:N, :].rearrange("(p c) f -> p (c f)", p=1),
                          x[FULL:FULL + 1, 0:LAST * D]).then_inc(stored, 16)
            act.wait_ge(stored, 16 * (2 * NCH + 1))

        @block.vector
        def _(dve):
            V = nc.vector
            own = Steps(dve, dve_step)

            def clear(t, value=0.0):
                V.memset(t, value).then_inc(cleared, 1)

            clear(zeros[:, :])
            clear(ew[:, ET:])
            clear(attr2[:, 2 * ET:])
            clear(attr8[:, T2 * ET:])
            clear(eps[:, :], EPS)
            clear(key[:, :])
            clear(raw[:, :])
            clear(small[:, :])
            clear(msgs[0][:, :])

            def spread(ap, f=D):
                return ap[:, :, None].to_broadcast([P, ap.shape[1], f])


            def part_mean(feats, m):
                dve.sem_inc(dve_go, 1)
                own.did(V.tensor_reduce(m, v3(feats), AX.X, ALU.add))

            def part_center(feats, hs, m, done):
                V.scalar_tensor_tensor(v3(hs), spread(m), -1.0 / D, v3(feats), ALU.mult, ALU.add).then_inc(done, 1)

            def part_var(n, c):
                dve.wait_ge(n["square"], c + 1)
                V.tensor_reduce(var, v3(tD), AX.X, ALU.add).then_inc(n["varsum"], 1)

            def part_scale(n, c, hs):
                dve.wait_ge(n["sdev"], c + 1)
                own.did(V.reciprocal(inv, sdev))
                own.settle()
                V.scalar_tensor_tensor(v3(hs), v3(hs), 0.0, spread(inv), ALU.max, ALU.mult).then_inc(n["norm"], 1)

            def step_of(t, c):
                return t[:, bass.ds(c * CW, CW)]

            def normalize_twice(c, new=True, middle=True, old=True, early=False):
                n = nd[2]
                own.begin(c - BEHIND if new and middle and old and not early else 0, new + 3 * middle + old)
                if new:
                    dve.wait_ge(n["takenB"], c + 1)
                    if middle:
                        dve.wait_ge(n["center"], c)
                    part_mean(step_of(x, c), mean)
                if old:
                    dve.wait_ge(n["square2"], c - 1)
                    own.did(V.tensor_reduce(var2, v3(tC), AX.X, ALU.add))
                if middle:
                    dve.wait_ge(n["square"], c)
                    own.did(V.tensor_reduce(var, v3(tD), AX.X, ALU.add))
                own.settle()
                if old:
                    V.scalar_tensor_tensor(total2, var2, 1.0 / D, floor2, ALU.mult, ALU.add).then_inc(n["varsum2"], 1)
                if new:
                    part_center(step_of(x, c), step_of(h, c), mean, n["center"])
                if middle:
                    dve.wait_ge(n["relu"], c)
                    if old:
                        dve.wait_ge(n["center2"], c - 1)
                        dve.wait_ge(n["varsum2"], c - 1)
                    own.did(V.tensor_reduce(mean2, v3(uA), AX.X, ALU.add))
                    own.did(V.tensor_scalar(floor2, var, EPS / D, EPS * EPS, ALU.mult, ALU.add))
                    own.settle()
                if old:
                    dve.wait_ge(n["sdev2"], c - 1)
                    if not early:
                        dve.wait_ge(n["norm2"], c - 2)
                    V.reciprocal(inv2, sdev2).then_inc(n["inv2"], 1)
                if middle:
                    part_center(uA, step_of(h, c - 1), mean2, n["center2"])

            def node_phase(d):
                n = nd[d]

                def enter(c):
                    if d > 1:
                        dve.wait_ge(n["takenB"], c + 1)

                def clip(c):
                    dve.wait_ge(n["relu"], c + 1)
                    own.did(V.scalar_tensor_tensor(step_of(x, c), tC, 1.0, step_of(x, c), ALU.min, ALU.add))
                    own.settle()

                def head(c, first=False):
                    if not first:
                        dve.wait_ge(n["center"], c)
                    part_mean(step_of(x, c), mean)
                    own.settle()
                    if d == 0:
                        V.tensor_scalar(mean, mean, 1.0 / D, None, ALU.mult).then_inc(n["mean"], 1)

                def body(c):
                    enter(c)
                    if d == 1:
                        clip(c)
                        part_var(n, c - 1)
                        head(c)
                        part_scale(n, c - 1, step_of(h, c - 1))
                        part_center(step_of(x, c), step_of(h, c), mean, n["center"])
                    elif d == 0:
                        head(c)
                        part_var(n, c - 1)
                        part_scale(n, c - 1, step_of(h, c - 1))
                    else:
                        head(c)
                        part_var(n, c - 1)
                        part_center(step_of(x, c), step_of(h, c), mean, n["center"])
                        part_scale(n, c - 1, step_of(h, c - 1))

                if d == 0:
                    dve.wait_ge(cleared, CLEARED)
                    dve.wait_ge(x_first, 16 * 3)
                else:
                    to, sums = (uA, uB) if d == 1 else (x[:, 0:CW], x[:, 0:CW])
                    if d == 1:
                        dve.wait_ge(n["looped"], 1)
                    dve.wait_ge(n["loadA"], 16)
                    V.tensor_tensor(to, to, tA[:, :], ALU.add).then_inc(n["takenA"], 1)
                    dve.wait_ge(n["loadB"], 16)
                    dve.wait_ge(n["takenA"], 1)
                    V.tensor_tensor(sums, to, tB[:, :], ALU.add).then_inc(n["takenB"], 1)
                if d == 2:
                    normalize_twice(0, middle=False, old=False)
                    own.end(1)
                    normalize_twice(1, old=False)
                    own.end(1)
                    normalize_twice(2, early=True)
                    own.end(1)
                    with dve.Fori(BEHIND, NCH) as c:
                        normalize_twice(c)
                    own.end(NCH - BEHIND)
                    normalize_twice(NCH, new=False)
                    own.end(1)
                    normalize_twice(NCH + 1, new=False, middle=False)
                    own.end(1)
                    dve.wait_ge(n["norm2"], NCH)
                    return
                own.begin(0, own_peeled[d][0])
                enter(0)
                if d == 1:
                    clip(0)
                head(0, True)
                if d:
                    part_center(step_of(x, 0), step_of(h, 0), mean, n["center"])
                own.end(1)
                if d == 0:
                    dve.wait_ge(x_loaded, 16 * 4)
                with dve.Fori(1, NCH) as c:
                    own.begin(c - 1, own_turn[d])
                    body(c)
                own.end(NCH - 1)
                own.begin(0, own_peeled[d][1])
                part_var(n, NCH - 1)
                part_scale(n, NCH - 1, step_of(h, NCH - 1))
                own.end(1)
                dve.wait_ge(n["norm"], NCH)

            def stage(l, par, col):
                return V.tensor_copy(gidx[par][:, :], GATHER[l][:, bass.ds(col, U)])

            def messages(l, c, par, col):
                e = ed[l]
                if l == 0:
                    own.did(V.tensor_tensor(v3(basis[:, :]), v3(rows[par][:, 0:U * D]),
                                            spread(ew[:, bass.ds(col, U)]), ALU.mult))
                    own.settle()
                    V.tensor_tensor(v3(raw[:, :]), v3(basis[:, :]), w0[:, None, :].to_broadcast([P, U, D]),
                                    ALU.mult).then_inc(e["raw"], 1)
                elif l == 1:
                    uv = attr2[:, bass.ds(col * 2, 2 * U)]
                    hats = small[:, 0:8 * U]
                    for k in range(4):
                        own.did(V.tensor_scalar(v3(hats, 4)[:, :, k], uv, -1.0 + 2.0 * k / 3.0, 1.5,
                                                ALU.subtract, ALU.mult))
                    own.settle()
                    own.did(V.scalar_tensor_tensor(hats, hats, -1.0, hats, ALU.mult, ALU.min))
                    own.settle()
                    own.did(V.tensor_scalar(hats, hats, 1.0, 0.0, ALU.add, ALU.max))
                    own.settle()
                    hv = hats.rearrange("p (u c n) -> p u c n", c=2, n=4)
                    own.did(V.tensor_tensor(basis[:, :].rearrange("p (u a b) -> p u a b", a=4, b=4),
                                            hv[:, :, 0, :, None].to_broadcast([P, U, 4, 4]),
                                            hv[:, :, 1, None, :].to_broadcast([P, U, 4, 4]), ALU.mult))
                    own.settle()
                    for m in range(7):
                        dve.wait_ge(e["prod"], 14 * c + (7 * par + m + 1))
                        V.tensor_tensor(v3(prod[:, m * 512:(m + 1) * 512]), v3(psP[m % 2][:, :]),
                                        spread(basis[:, 32 * m:32 * m + 32]), ALU.mult).then_inc(e["used"], 1)
                    dve.wait_ge(e["used"], 14 * c + (7 * par + 7))
                    V.tensor_reduce(v3(raw[:, :]), prod[:, :].rearrange("p (u k o) -> p u o k", k=D, o=D),
                                    AX.X, ALU.add).then_inc(e["raw"], 1)
                elif l == 2:
                    dve.wait_ge(rev_in[par], 16 * c + 16)
                    for m in range(8):
                        s, q = m // 4, m % 4
                        tiles = min(4, U - 4 * q)
                        dve.wait_ge(e["prod"], 16 * c + (8 * par + m + 1))
                        o = s * CW + q * 288
                        ps = psP[m % 2][:, 0:tiles * 72].rearrange("p (u t o) -> p u t o", t=A9, o=HALF)
                        pr = prod[:, o:o + tiles * 72].rearrange("p (u t o) -> p u t o", t=A9, o=HALF)
                        at = (rev8[par][:, 4 * q * T2:(4 * q + tiles) * T2] if s
                              else attr8[:, bass.ds(col * T2 + 4 * q * T2, T2 * tiles)])
                        V.tensor_tensor(pr[:, :, 0:T2, :], ps[:, :, 0:T2, :],
                                        v3(at, T2)[:, :, :, None].to_broadcast([P, tiles, T2, HALF]), ALU.mult)
                        V.tensor_copy(pr[:, :, T2, :], ps[:, :, T2, :]).then_inc(e["used"], 1)
                    dve.wait_ge(e["used"], 16 * c + (8 * par + 8))
                    for s in range(2):
                        k = V.tensor_reduce(v3(raw[:, :])[:, :, s * HALF:(s + 1) * HALF],
                                            prod[:, s * CW:s * CW + U * 72]
                                            .rearrange("p (u t o) -> p u o t", t=A9, o=HALF), AX.X, ALU.add)
                    k.then_inc(e["raw"], 1)
                else:
                    for m in range(4):
                        tiles = min(4, U - 4 * m)
                        dve.wait_ge(e["prod"], 8 * c + (4 * par + m + 1))
                        av = v3(attr8[:, bass.ds(col * T2 + 4 * m * T2, T2 * tiles)], T2)[:, :, :, None]
                        V.tensor_tensor(prod[:, m * 512:m * 512 + tiles * P]
                                        .rearrange("p (u j h) -> p u j h", j=T2, h=D),
                                        psP[m % 2][:, 0:tiles * P].rearrange("p (u j h) -> p u j h", j=T2, h=D),
                                        av.to_broadcast([P, tiles, T2, D]), ALU.mult).then_inc(e["used"], 1)
                    dve.wait_ge(e["used"], 8 * c + (4 * par + 4))
                    V.tensor_reduce(v3(basis[:, :]), prod[:, 0:CW].rearrange("p (u j h) -> p u h j", j=T2, h=D),
                                    AX.X, ALU.add).then_inc(e["preact"], 1)

            def edge_phase(l):
                e = ed[l]
                if l == 2:
                    dve.wait_ge(weights, WEIGHTS)
                for par in range(2):
                    stage(l, par, par * U).then_inc(e["staged"], 1)

                def equal(g):
                    V.tensor_copy(key[:, :], KEY[l][:, bass.ds(g * U, U)]).then_inc(e["key"], 1)
                    dve.wait_ge(e["keyT"], g + 1)
                    V.tensor_tensor(v3(same[:, :], P), v3(psK[:, 0:CW], P), spread(key[:, :], P), ALU.is_equal)\
                        .then_inc(e["same"], 1)

                equal(0)
                with dve.Fori(0, PAIRS) as c:
                    own.begin(c, STEPS[l])
                    for par in range(2):
                        col = (2 * c + par) * U
                        dve.wait_ge(gath[l][par], c * GATH + GATH)
                        stage(l, par, col + AHEAD * U)
                        messages(l, c, par, col)
                        if l < 2:
                            dve.wait_ge(e["same"], 2 * c + (par + 1))
                            if l == 1:
                                dve.wait_ge(e["raw"], 2 * c + (par + 1))
                            before, first = small[:, 0:U], small[:, U:2 * U]
                            own.did(V.tensor_tensor(v3(prod[:, 0:CW], P), v3(same[:, :], P),
                                                    lower[:, None, :].to_broadcast([P, U, P]), ALU.mult))
                            own.did(V.tensor_scalar(first, key[:, :], pad_row[:, :], None, ALU.subtract))
                            own.settle()
                            own.did(V.tensor_reduce(before, v3(prod[:, 0:CW], P), AX.X, ALU.add))
                            own.settle()
                            own.did(V.scalar_tensor_tensor(first, before, 0.0, first, ALU.is_equal, ALU.mult))
                            own.settle()
                            own.did(V.tensor_scalar(sidx[par][:, :], first, pad_row[:, :], None, ALU.add))
                            own.settle()
                            own.did(V.tensor_copy(TO[l][:, bass.ds(col, U)], sidx[par][:, :]))
                        else:
                            own.did(V.tensor_copy(sidx[par][:, :], TO[l][:, bass.ds(col, U)]))
                            if l == 2:
                                root(c, par)
                        dve.wait_ge(e["sum"], 2 * c + (par + 1))
                        V.tensor_copy(msgs[par][:, :], psM[:, 0:U * D]).then_inc(e["msg"], 1)
                        equal(2 * c + (par + 1))
                        for s in range(2):
                            dve.wait_ge(scat[l][s], c * (2 * SCAT) + (FREE + par * SCAT))
                own.end(PAIRS)

            def root(c, par):
                w = RB * P
                xs = x[:, bass.ds(c * w, w)]
                if par == 0:
                    own.did(V.tensor_tensor(v3(xs), v3(xs), bias16[:, None, :].to_broadcast([P, RB * 8, D]), ALU.add))
                else:
                    dve.wait_ge(root_s["root"], c + 1)
                    own.did(V.tensor_tensor(xs, xs, psK[:, 0:w], ALU.add))
                own.settle()

            for l in range(4):
                node_phase(l)
                if l == 0:
                    dve.wait_ge(loaded, LOADS)
                    own.begin(0, 2)
                    own.did(V.tensor_copy(pad_row[:, :], dst[:, ICOLS - 1:ICOLS]))
                    own.did(V.tensor_scalar_add(slw1[:, :], slw1[:, :], 1.0))
                    own.settle()
                    own.end(1)
                edge_phase(l)
                if l == 1:
                    dve.wait_ge(w4_psum, 1)
                    for v in range(8):
                        k = V.tensor_scalar(W4[:, v * 256:(v + 1) * 256], psM[:, 0:256], rowmask[:, v:v + 1], NORM_LIN,
                                            ALU.mult, ALU.mult)
                    k.then_inc(w4_ready, 1)

            def halved(c, q):
                dve.wait_ge(up["half"], c * QUADS + (q + 1))
                k = V.tensor_reduce(v3(tD[:, 64 * q:64 * q + 64]), products(q)[1].rearrange("p u i k -> p u k i"),
                                    AX.X, ALU.add)
                if (q + 1) % (QUADS // 2) == 0:
                    k.then_inc(up["preact"], 1)

            def update(c, first):
                for q in range(QUADS):
                    dve.wait_ge(up["prod"], c * QUADS + (q + 1))
                    V.tensor_tensor(v3(wide[q % DEEP]), v3(psQ[q % 2]), spread(h[:, bass.ds(c * CW + 64 * q, 64)]),
                                    ALU.mult).then_inc(up["used"], 1)
                    if q >= LAG:
                        if q == LAG and not first:
                            dve.wait_ge(up["silu"], 2 * c - 1)
                        if q == LAG + QUADS // 2 and not first:
                            dve.wait_ge(up["silu"], 2 * c)
                        halved(c, q - LAG)
                    elif not first:
                        halved(c - 1, QUADS + q - LAG)

            dve.wait_ge(up["loadA"], 16)
            dve.wait_ge(up["loadB"], 16)
            V.tensor_tensor(tA[:, :], tA[:, :], tB[:, :], ALU.add).then_inc(up["total"], 1)
            update(0, True)
            with dve.Fori(1, NCH) as c:
                update(c, False)
            for q in range(QUADS - LAG, QUADS):
                halved(NCH - 1, q)
            dve.wait_ge(up["resid"], NCH)
            dve.wait_ge(up["update"], NCH)
            xs = x[:, (NCH - 1) * CW:]
            V.scalar_tensor_tensor(xs, psK[:, 0:CW], NORM_LIN, xs, ALU.mult, ALU.add).then_inc(up["done"], 1)


_INS = ["x", "src", "dst", "edge_attr_2", "edge_attr_8", "edge_attr_8_reversed", "edge_weight", "L0_gnn_weight",
        "L0_gnn_self_loop_weight", "L1_gnn_weight", "L2_gnn_ln_g_n", "L2_gnn_ln_b_n", "L2_gnn_We_n",
        "L2_gnn_be_n", "L2_gnn_Wr_n", "L2_gnn_b_n", "L2_gnn_ln_g_r", "L2_gnn_ln_b_r", "L2_gnn_We_r",
        "L2_gnn_be_r", "L2_gnn_Wr_r", "L2_gnn_b_r", "L3_gnn_W_msg_tp", "L3_gnn_W_msg_lin",
        "L3_gnn_W_upd_tp", "L3_gnn_W_upd_lin"]


def kernel(**inputs):
    import numpy as _np
    import concourse.bacc as _bacc
    from concourse import mybir as _mybir
    from concourse.bass_utils import run_bass_kernel_spmd as _run

    nc = _bacc.Bacc("TRN2", target_bir_lowering=False, num_devices=1)
    inputs["edge_attr_8_reversed"] = _np.ascontiguousarray(_np.asarray(inputs["edge_attr_8"])[::-1])
    arrays, args = {}, []
    for name in _INS:
        a = _np.ascontiguousarray(inputs[name])
        a = a.reshape(a.shape or (1,))
        arrays[f"in_{name}_dram"] = a
        args.append(nc.dram_tensor(f"in_{name}_dram", a.shape, _mybir.dt.from_np(a.dtype), kind="ExternalInput").ap())
    out = nc.dram_tensor("out_0_dram", (N, D), _mybir.dt.float32, kind="ExternalOutput").ap()
    build_gnn(nc, *args, out)
    r = _run(nc, [arrays], core_ids=[0])
    return r.results[0]["out_0_dram"]
```
